# Optimizing a Trainium2 kernel written in Bass

```python
import numpy as np
import jax
import jax.numpy as jnp

def _softmax(x, axis=-1):
    return jax.nn.softmax(x, axis=axis)

def _gelu(x):
    return jax.nn.gelu(x, approximate=True)

def _silu(x):
    return jax.nn.silu(x)

def _sigmoid(x):
    return jax.nn.sigmoid(x)

def _layernorm(x, axis=-1, eps=1e-05):
    m = jnp.mean(x, axis=axis, keepdims=True)
    v = jnp.var(x, axis=axis, keepdims=True)
    return (x - m) / jnp.sqrt(v + eps)

def _scatter_add(tgt, idx, src, axis=0):
    return tgt.at[idx].add(src)

def _segment_sum(src, seg, n):
    return jax.ops.segment_sum(src, seg, n)
kernel_name = 'mk_prb_d1_jaxref_r8_3805f0'

def setup_inputs(seed: int=0):
    np.random.seed(seed)
    _w = jnp.asarray

    def _L0_attn_setup():
        import jax, jax.numpy as jnp
        import numpy as np
        import math
        N, S, E, H = (4, 512, 128, 16)
        D = E // H
        key = jax.random.key(seed)
        ks = jax.random.split(key, 9)
        w = 1.0 / math.sqrt(E)
        mk = lambda k, shape: jax.random.normal(k, shape, jnp.float32) * w
        return {'x': jax.random.normal(ks[0], (N, S, E), jnp.float32), 'Wq': mk(ks[1], (E, E)), 'bq': mk(ks[2], (E,)), 'Wk': mk(ks[3], (E, E)), 'bk': mk(ks[4], (E,)), 'Wv': mk(ks[5], (E, E)), 'bv': mk(ks[6], (E,)), 'Wo': mk(ks[7], (E, E)), 'bo': mk(ks[8], (E,))}
    _L0_attn_in = _L0_attn_setup()

    def _L0_ffn_setup():
        import jax, jax.numpy as jnp
        import numpy as np
        DIM = 128
        DEPTH = 2
        HEADS = 8
        DIM_HEAD = 64
        WINDOW = 64
        INNER = HEADS * DIM_HEAD
        HID = int(DIM * 4 * 2 / 3)
        B, N = (2, 1024)
        QK_SCALE = 8.0

        def shift_token(t):
            t1, t2 = jnp.split(t, 2, axis=-1)
            t2 = jnp.pad(t2, ((0, 0), (1, 0), (0, 0)))[:, :-1]
            return jnp.concatenate([t1, t2], axis=-1)

        def l2norm(t):
            return t / jnp.clip(jnp.linalg.norm(t, axis=-1, keepdims=True), 1e-12)

        def rotate_half(x):
            x1, x2 = jnp.split(x, 2, axis=-1)
            return jnp.concatenate([-x2, x1], axis=-1)

        def rotary_xpos(q, k):
            n = q.shape[-2]
            half_idx = jnp.arange(0, DIM_HEAD, 2, dtype=jnp.float32)
            inv_freq = 1.0 / 10000.0 ** (half_idx / DIM_HEAD)
            t = jnp.arange(n, dtype=jnp.float32)
            freqs = t[:, None] * inv_freq[None, :]
            freqs = jnp.concatenate([freqs, freqs], axis=-1)
            base = (half_idx + 0.4 * DIM_HEAD) / (1.4 * DIM_HEAD)
            power = (t - n // 2) / float(WINDOW // 2)
            scale = base[None, :] ** power[:, None]
            scale = jnp.concatenate([scale, scale], axis=-1)
            cos, sin = (jnp.cos(freqs), jnp.sin(freqs))
            q = q * cos * scale + rotate_half(q) * sin * scale
            k = k * cos / scale + rotate_half(k) * sin / scale
            return (q, k)

        def local_attention(q, k, v):
            b, h, n, d = q.shape
            w = n // WINDOW
            bq = q.reshape(b, h, w, WINDOW, d) * QK_SCALE
            bk = k.reshape(b, h, w, WINDOW, d)
            bv = v.reshape(b, h, w, WINDOW, d)

            def look_around(t):
                p = jnp.pad(t, ((0, 0), (0, 0), (1, 0), (0, 0), (0, 0)))
                return jnp.concatenate([p[:, :, :w], p[:, :, 1:]], axis=3)
            bk, bv = (look_around(bk), look_around(bv))
            bt = jnp.arange(n).reshape(w, WINDOW)
            btp = jnp.pad(bt, ((1, 0), (0, 0)), constant_values=-1)
            btk = jnp.concatenate([btp[:w], btp[1:]], axis=1)
            sim = jnp.einsum('bhwid,bhwjd->bhwij', bq, bk)
            i = bt[:, :, None]
            j = btk[:, None, :]
            mask = (i < j) | (i > j + WINDOW) | (j == -1)
            sim = jnp.where(mask, -jnp.finfo(sim.dtype).max, sim)
            attn = jax.nn.softmax(sim, axis=-1)
            out = jnp.einsum('bhwij,bhwjd->bhwid', attn, bv)
            return out.reshape(b, h, n, d)

        def _layer(x, wqkv, qs, ksc, wo, lg, lb, w1, b1, w2, b2):
            b, n, _ = x.shape
            h = shift_token(x)
            qkv = h @ wqkv
            q, k, v = jnp.split(qkv, 3, axis=-1)
            to_heads = lambda t: t.reshape(b, n, HEADS, DIM_HEAD).transpose(0, 2, 1, 3)
            q, k, v = (to_heads(q), to_heads(k), to_heads(v))
            q = l2norm(q) * qs
            k = l2norm(k) * ksc
            q, k = rotary_xpos(q, k)
            o = local_attention(q, k, v)
            o = o.transpose(0, 2, 1, 3).reshape(b, n, INNER)
            x = x + o @ wo
            h = shift_token(x)
            mu = h.mean(-1, keepdims=True)
            var = h.var(-1, keepdims=True)
            h = (h - mu) / jnp.sqrt(var + 1e-05) * lg + lb
            h = h @ w1 + b1
            a, g = jnp.split(h, 2, axis=-1)
            h = a * jax.nn.gelu(g, approximate=False)
            x = x + h @ w2 + b2
            return x
        key = jax.random.key(seed)
        ks = jax.random.split(key, 6)
        return {'x': jax.random.normal(ks[0], (B, N, DIM), jnp.float32), 'wqkv': jax.random.normal(ks[1], (DEPTH, DIM, 3 * INNER), jnp.float32) * 0.02, 'q_scale': jnp.ones((DEPTH, DIM_HEAD), jnp.float32), 'k_scale': jnp.ones((DEPTH, DIM_HEAD), jnp.float32), 'wo': jax.random.normal(ks[2], (DEPTH, INNER, DIM), jnp.float32) * 0.02, 'ln_g': jnp.ones((DEPTH, DIM), jnp.float32), 'ln_b': jnp.zeros((DEPTH, DIM), jnp.float32), 'w1': jax.random.normal(ks[3], (DEPTH, DIM, 2 * HID), jnp.float32) * 0.02, 'b1': jnp.zeros((DEPTH, 2 * HID), jnp.float32), 'w2': jax.random.normal(ks[4], (DEPTH, HID, DIM), jnp.float32) * 0.02, 'b2': jnp.zeros((DEPTH, DIM), jnp.float32)}
    _L0_ffn_in = _L0_ffn_setup()
    _d = {'L0_attn_x': _L0_attn_in['x'], 'L0_attn_Wq': _L0_attn_in['Wq'], 'L0_attn_bq': _L0_attn_in['bq'], 'L0_attn_Wk': _L0_attn_in['Wk'], 'L0_attn_bk': _L0_attn_in['bk'], 'L0_attn_Wv': _L0_attn_in['Wv'], 'L0_attn_bv': _L0_attn_in['bv'], 'L0_attn_Wo': _L0_attn_in['Wo'], 'L0_attn_bo': _L0_attn_in['bo'], 'L0_ffn_wqkv': _L0_ffn_in['wqkv'], 'L0_ffn_q_scale': _L0_ffn_in['q_scale'], 'L0_ffn_k_scale': _L0_ffn_in['k_scale'], 'L0_ffn_wo': _L0_ffn_in['wo'], 'L0_ffn_ln_g': _L0_ffn_in['ln_g'], 'L0_ffn_ln_b': _L0_ffn_in['ln_b'], 'L0_ffn_w1': _L0_ffn_in['w1'], 'L0_ffn_b1': _L0_ffn_in['b1'], 'L0_ffn_w2': _L0_ffn_in['w2'], 'L0_ffn_b2': _L0_ffn_in['b2']}
    _x0 = _d['L0_attn_x']
    _d['L0_attn_x'] = jax.random.normal(jax.random.fold_in(jax.random.key(seed), 1), (16, 512, 128), dtype=_x0.dtype)
    del _x0
    return _d

def reference(L0_attn_x, L0_attn_Wq, L0_attn_bq, L0_attn_Wk, L0_attn_bk, L0_attn_Wv, L0_attn_bv, L0_attn_Wo, L0_attn_bo, L0_ffn_wqkv, L0_ffn_q_scale, L0_ffn_k_scale, L0_ffn_wo, L0_ffn_ln_g, L0_ffn_ln_b, L0_ffn_w1, L0_ffn_b1, L0_ffn_w2, L0_ffn_b2):

    def _L0_attn_ref(x, Wq, bq, Wk, bk, Wv, bv, Wo, bo):
        import jax, jax.numpy as jnp
        import numpy as np
        import math
        N, S, E, H = (4, 512, 128, 16)
        D = E // H
        n, s, e = x.shape
        h, d = (H, D)
        scale = 1.0 / math.sqrt(d)

        def proj(W, b):
            y = jnp.einsum('nse,fe->nsf', x, W) + b
            return y.reshape(n, s, h, d).transpose(0, 2, 1, 3)
        Q = proj(Wq, bq)
        K = proj(Wk, bk)
        V = proj(Wv, bv)
        scores = jnp.einsum('nqhd,nkhd->nhqk', Q, K) * scale
        attn = jax.nn.softmax(scores, axis=-1)
        out = jnp.einsum('nhql,nlhd->nqhd', attn, V)
        out = out.reshape(n, s, e)
        return jnp.einsum('nse,fe->nsf', out, Wo) + bo

    def _L0_ffn_ref(x, wqkv, q_scale, k_scale, wo, ln_g, ln_b, w1, b1, w2, b2):
        import jax, jax.numpy as jnp
        import numpy as np
        DIM = 128
        DEPTH = 2
        HEADS = 8
        DIM_HEAD = 64
        WINDOW = 64
        INNER = HEADS * DIM_HEAD
        HID = int(DIM * 4 * 2 / 3)
        B, N = (2, 1024)
        QK_SCALE = 8.0

        def shift_token(t):
            t1, t2 = jnp.split(t, 2, axis=-1)
            t2 = jnp.pad(t2, ((0, 0), (1, 0), (0, 0)))[:, :-1]
            return jnp.concatenate([t1, t2], axis=-1)

        def l2norm(t):
            return t / jnp.clip(jnp.linalg.norm(t, axis=-1, keepdims=True), 1e-12)

        def rotate_half(x):
            x1, x2 = jnp.split(x, 2, axis=-1)
            return jnp.concatenate([-x2, x1], axis=-1)

        def rotary_xpos(q, k):
            n = q.shape[-2]
            half_idx = jnp.arange(0, DIM_HEAD, 2, dtype=jnp.float32)
            inv_freq = 1.0 / 10000.0 ** (half_idx / DIM_HEAD)
            t = jnp.arange(n, dtype=jnp.float32)
            freqs = t[:, None] * inv_freq[None, :]
            freqs = jnp.concatenate([freqs, freqs], axis=-1)
            base = (half_idx + 0.4 * DIM_HEAD) / (1.4 * DIM_HEAD)
            power = (t - n // 2) / float(WINDOW // 2)
            scale = base[None, :] ** power[:, None]
            scale = jnp.concatenate([scale, scale], axis=-1)
            cos, sin = (jnp.cos(freqs), jnp.sin(freqs))
            q = q * cos * scale + rotate_half(q) * sin * scale
            k = k * cos / scale + rotate_half(k) * sin / scale
            return (q, k)

        def local_attention(q, k, v):
            b, h, n, d = q.shape
            w = n // WINDOW
            bq = q.reshape(b, h, w, WINDOW, d) * QK_SCALE
            bk = k.reshape(b, h, w, WINDOW, d)
            bv = v.reshape(b, h, w, WINDOW, d)

            def look_around(t):
                p = jnp.pad(t, ((0, 0), (0, 0), (1, 0), (0, 0), (0, 0)))
                return jnp.concatenate([p[:, :, :w], p[:, :, 1:]], axis=3)
            bk, bv = (look_around(bk), look_around(bv))
            bt = jnp.arange(n).reshape(w, WINDOW)
            btp = jnp.pad(bt, ((1, 0), (0, 0)), constant_values=-1)
            btk = jnp.concatenate([btp[:w], btp[1:]], axis=1)
            sim = jnp.einsum('bhwid,bhwjd->bhwij', bq, bk)
            i = bt[:, :, None]
            j = btk[:, None, :]
            mask = (i < j) | (i > j + WINDOW) | (j == -1)
            sim = jnp.where(mask, -jnp.finfo(sim.dtype).max, sim)
            attn = jax.nn.softmax(sim, axis=-1)
            out = jnp.einsum('bhwij,bhwjd->bhwid', attn, bv)
            return out.reshape(b, h, n, d)

        def _layer(x, wqkv, qs, ksc, wo, lg, lb, w1, b1, w2, b2):
            b, n, _ = x.shape
            h = shift_token(x)
            qkv = h @ wqkv
            q, k, v = jnp.split(qkv, 3, axis=-1)
            to_heads = lambda t: t.reshape(b, n, HEADS, DIM_HEAD).transpose(0, 2, 1, 3)
            q, k, v = (to_heads(q), to_heads(k), to_heads(v))
            q = l2norm(q) * qs
            k = l2norm(k) * ksc
            q, k = rotary_xpos(q, k)
            o = local_attention(q, k, v)
            o = o.transpose(0, 2, 1, 3).reshape(b, n, INNER)
            x = x + o @ wo
            h = shift_token(x)
            mu = h.mean(-1, keepdims=True)
            var = h.var(-1, keepdims=True)
            h = (h - mu) / jnp.sqrt(var + 1e-05) * lg + lb
            h = h @ w1 + b1
            a, g = jnp.split(h, 2, axis=-1)
            h = a * jax.nn.gelu(g, approximate=False)
            x = x + h @ w2 + b2
            return x
        for l in range(DEPTH):
            x = _layer(x, wqkv[l], q_scale[l], k_scale[l], wo[l], ln_g[l], ln_b[l], w1[l], b1[l], w2[l], b2[l])
        return x
    x = L0_attn_x
    xn = _layernorm(x, axis=-1)
    x = x + _L0_attn_ref(xn, L0_attn_Wq, L0_attn_bq, L0_attn_Wk, L0_attn_bk, L0_attn_Wv, L0_attn_bv, L0_attn_Wo, L0_attn_bo) + _L0_ffn_ref(xn, L0_ffn_wqkv, L0_ffn_q_scale, L0_ffn_k_scale, L0_ffn_wo, L0_ffn_ln_g, L0_ffn_ln_b, L0_ffn_w1, L0_ffn_b1, L0_ffn_w2, L0_ffn_b2)
    return x

_drawn_inputs = setup_inputs


def setup_inputs(seed=0):
    import zlib

    import numpy as np

    out = dict(_drawn_inputs(seed))
    spreads = {'L0_ffn_q_scale': (1.0, 0.6),
     'L0_ffn_k_scale': (1.0, 0.6),
     'L0_ffn_ln_g': (1.0, 0.6),
     'L0_ffn_ln_b': (0.0, 0.8),
     'L0_ffn_b1': (0.0, 0.8),
     'L0_ffn_b2': (0.0, 0.45)}
    factors = {'L0_attn_bq': 29.181,
     'L0_attn_bk': 26.732,
     'L0_attn_bv': 26.88,
     'L0_ffn_wqkv': 3.79,
     'L0_ffn_wo': 3.79,
     'L0_ffn_w1': 6.274,
     'L0_ffn_w2': 6.183,
     'L0_attn_Wq': 2.897,
     'L0_attn_Wk': 2.807,
     'L0_attn_bo': 8.0}
    for name, (base, spread) in spreads.items():
        noise = np.random.default_rng([zlib.crc32(name.encode()), seed]).standard_normal(out[name].shape)
        drawn = base * np.exp(spread * noise) if base else spread * noise
        out[name] = jnp.asarray(drawn.astype(out[name].dtype))
    for name, factor in factors.items():
        out[name] = (out[name] * factor).astype(out[name].dtype)
    return out
```

```python
from contextlib import ExitStack

import concourse.bass as bass
from concourse import mybir

ALU = mybir.AluOpType
ACT = mybir.ActivationFunctionType
AX_X = mybir.AxisListType.X
F32 = mybir.dt.float32
F32R = mybir.dt.float32r
BF16 = mybir.dt.bfloat16

P = 128
B, S, E = 16, 512, 128
NB = S // P
H, D = 16, 8
DEPTH, LH, LD, WIN = 2, 8, 64, 64
INNER = LH * LD
NPAIR = LH // 2
NW = S // WIN
HW = NW // 2
HID = 341
HT = 3
QK_SCALE = 8.0
EPS = 1e-5
TINY = 1e-24
MASKED = -2.0 ** 124
RING = 8
SCALE = float(D) ** -0.5


def schedule():
    steps = [("norm_x",), ("qkv_full", 0), ("qkv_full", 1), ("qkv_full", 2), ("qkv_full", 3), ("shift", 0)]
    local = []
    for l in range(DEPTH):
        a = [[] for _ in range(21)]
        a[0] = [("project", l, 0), ("project", l, 1), ("rope", l, 0)]
        a[1] = [("rope", l, 1), ("qk_t", l, 0), ("project", l, 2)]
        a[2] = [("scores", l, 0), ("rope", l, 2), ("qk_t", l, 1), ("project", l, 3)]
        a[3] = [("scores", l, 1), ("rope", l, 3)]
        for u in range(4, 14):
            if u >= 6:
                a[u].append(("values", l, u - 6))
            if u < 12:
                a[u].append(("probs_t", l, u - 4))
            if u < 10:
                a[u].append(("scores", l, u - 2))
            if u < 6:
                a[u].append(("qk_t", l, u - 2))
        a[14] = [("out_local", l)]
        a[15] = [("center", l)]
        a[16] = [("variance", l)]
        a[17] = [("spread", l)]
        a[18] = [("up", l, 0), ("up", l, 1)]
        a[19] = [("up", l, 2)]
        a[20] = [("down", l)] + ([("shift", l + 1)] if l + 1 < DEPTH else [])
        local += a
    full = {2: ("scores_full", 0), 7: ("values_full", 0), 11: ("scores_full", 1), 13: ("values_full", 1),
            16: ("scores_full", 2), 19: ("values_full", 2), 22: ("scores_full", 3), 26: ("values_full", 3)}
    for u in range(len(local)):
        steps += local[u]
        if u in full:
            steps.append(full[u])
        if u == 26:
            steps.append(("attn_load",))
        if u == 36:
            steps.append(("attn_t",))
    steps += [("attn_out",), ("final",)]
    return steps


STEPS = schedule()


def taker(step, k):
    kind = step[0]
    if kind in ("norm_x", "project", "center", "attn_t"):
        return "act"
    if kind == "qk_t":
        return ("act", "dve")[k]
    if kind == "scores":
        return "act"
    if kind == "up":
        return ("act", "dve")[k]
    if kind == "probs_t":
        return ("act", "dve")[step[2] % 2]
    if kind == "values":
        return ("dve", "act")[step[2] % 2]
    return "dve"


BANKS = {"norm_x": 1, "qkv_full": 1, "project": 3, "qk_t": 2, "scores": 1, "probs_t": 1, "values": 1, "out_local": 1,
         "center": 1, "variance": 1, "spread": 1, "up": 2, "down": 1, "attn_t": 1, "attn_out": 1, "final": 1}


def number_fills():
    fill, took, count = {}, [], {"act": 0, "dve": 0}
    for step in STEPS:
        for k in range(BANKS.get(step[0], 0)):
            fill[step, k] = len(took)
            who = taker(step, k)
            count[who] += 1
            took.append((who, count[who]))
    return fill, took, count


RECIP_AFTER = {("scores", l, d + 1): l * 8 + d for l in range(DEPTH) for d in range(7)}
RECIP_AFTER |= {("probs_t", l, 6): l * 8 + 7 for l in range(DEPTH)}
PREPS = 8 + 4 * DEPTH
FILL, TOOK, TAKEN = number_fills()
NF = len(TOOK)
CYCLE = -(-NF // RING) * RING
TOOK += [TOOK[n - RING] for n in range(NF, CYCLE)]


class Signal:

    def __init__(self, sem, per, ahead=0):
        self.sem, self.per, self.ahead = sem, per, ahead


class Count:

    def __init__(self, eng, i, signals):
        self.base = {}
        for signal in signals:
            if signal.per not in self.base:
                count = eng.alloc_register(f"{str(eng.engine).split('.')[-1]}_passes_times_{signal.per}")
                eng.reg_alu(count, i, signal.per, ALU.mult)
                self.base[signal.per] = eng.snap(count)

    def __call__(self, signal, n):
        assert n + signal.ahead > 0
        return self.base[signal.per] + (n + signal.ahead)


def build(nc, t, out):
    with ExitStack() as ctx:
        def sb(name, shape, dt=F32):
            return ctx.enter_context(nc.sbuf_tensor("sb_" + name, shape, dt))

        def sem(name, per=0, ahead=0):
            return Signal(ctx.enter_context(nc.semaphore(name)), per, ahead)

        w3h, w3l = sb("w3h", [P, 3 * E], F32R), sb("w3l", [P, 3 * E], F32R)
        wo_full = sb("wo_full", [P, E])
        wqh, wql = sb("wqh", [P, DEPTH, 3 * INNER], F32R), sb("wql", [P, DEPTH, 3 * INNER], F32R)
        wuh, wul = sb("wuh", [P, DEPTH, 2, HT * P], F32R), sb("wul", [P, DEPTH, 2, HT * P], F32R)
        wo_local = sb("wo_local", [P, DEPTH, NPAIR, E])
        wd = sb("wd", [P, DEPTH, HT, E])
        bias3 = sb("bias3", [P, 3 * E])
        bo = sb("bo", [P, 1])
        lng, lnb, b2 = sb("lng", [P, DEPTH]), sb("lnb", [P, DEPTH]), sb("b2", [P, DEPTH])
        b1 = sb("b1", [P, DEPTH, 2, HT])
        ident, centre = sb("ident", [P, P]), sb("centre", [P, P])
        ones, mean_of = sb("ones", [P, P]), sb("mean_of", [P, 1])
        identb, mask = sb("identb", [P, P], BF16), sb("mask", [P, 2, P], BF16)
        half = sb("half", [P, NB])
        tab = sb("tab", [P, DEPTH, 2, 2, NB, LD])

        xt, xr = sb("xt", [P, NB, E]), sb("xr", [P, NB, E])
        st, mv, mean = sb("st", [P, NB, 6]), sb("mv", [P, 3, NB]), sb("mean", [P, NB])
        ve4, rs4 = sb("ve4", [P, NB]), sb("rs4", [P, NB])
        xT = [sb(f"xT{k}", [P, S]) for k in range(2)]
        xT.append(xT[0])
        mh, ml = sb("mh", [P, S], F32R), sb("ml", [P, S], F32R)
        xh, xl = mh, ml
        gate, hid = sb("gate", [P, S]), sb("hid", [P, HT, S])
        sq2 = sb("sq2", [P, S])
        qkvf = sb("qkvf", [P, NB, 3, H, D])
        pr = sb("pr", [P, H * H * D])
        sf, ef = sb("sf", [P, H, H]), sb("ef", [P, H, H])
        nmf, sumf, rf = sb("nmf", [P, H]), sb("sumf", [P, H]), sb("rf", [P, H])
        of, ofs = sb("of", [P, H, D]), sb("ofs", [P, 2, H, D])
        orow = sb("orow", [P, NB, E])
        hh, hl = sb("hh", [P, S], F32R), sb("hl", [P, S], F32R)
        qk, sq = sb("qk", [P, 2, 1024]), sb("sq", [P, 1024])
        ssq, rn = sb("ssq", [P, 2, 16]), sb("rn", [P, 16])
        t2 = sb("t2", [P, 1024])
        qbd = sb("qbd", [P, 2, NPAIR, 2, 2, WIN])
        kT = sb("kT", [P, NPAIR, WIN + S])
        v, vs = sb("v", [P, NB, INNER]), sb("vs", [P, NB, INNER])
        nml, suml, rl = sb("nml", [P, 2, HW]), sb("suml", [P, 2, HW]), sb("rl", [P, 2, HW])
        pl = sb("pl", [P, 2, HW, P])
        pT = sb("pT", [P, 2, HW, P])
        oTl = sb("oTl", [P, NPAIR, S])
        x2 = sb("x2", [P, S])
        hs = sb("hs", [P, S])
        veps, rsq = sb("veps", [P, NB]), sb("rsq", [P, NB])
        hc, rs = sb("hc", [P, S]), sb("rs", [P, S])
        oT, rT, ob = sb("oT", [P, S]), sb("rT", [P, S]), xr
        stage = pr[:]
        stage2 = [qk[:, :, :].rearrange("p a b -> p (a b)"), oTl[:, :, :].rearrange("p a b -> p (a b)")]
        stage3 = v[:, :, :].rearrange("p a b -> p (a b)")
        scale_rows = stage[:, 384:896].rearrange("p (l a k d) -> p l a k d", l=DEPTH, a=2, k=2)

        ring = [ctx.enter_context(nc.psum_tensor(f"ring{k}", [P, S], F32)) for k in range(RING)]
        scratch = nc.dram_tensor("heads_scratch", (H, S, D), F32, kind="Internal").ap()

        s_w = sem("weights_loaded")
        s_w2 = sem("weights_loaded_2")
        s_set = sem("memory_set")
        s_prep = sem("weights_split")
        s_x = sem("x_loaded", 16)
        s_xr = sem("x_again_loaded", 16)
        s_stats = sem("stats_done", 4)
        s_rstd = sem("rstd_done", 1)
        s_xn = sem("xn_done", 1)
        filled = sem("ring_filled", NF)
        act_took = sem("act_took_bank", TAKEN["act"], TAKEN["act"])
        dve_took = sem("dve_took_bank", TAKEN["dve"], TAKEN["dve"])
        s_xh = sem("x_high_done", 1)
        s_xl = sem("x_low_done", 1)
        s_full = sem("full_attention_steps", 9 * NB)
        s_exp = sem("full_exponentials", NB)
        s_heads = [sem(f"heads_stored_{k}", 16 * NB // 2) for k in range(2)]
        s_orow = sem("heads_loaded", 16)
        s_hh = sem("h_high_done", DEPTH)
        s_hl = sem("h_low_done", DEPTH)
        s_sq = sem("squares_done", 4 * DEPTH)
        s_rot = sem("rotary_products", 4 * DEPTH)
        s_sin = sem("sine_products", 4 * DEPTH)
        s_ssq = sem("square_sums", 2 * 4 * DEPTH, 1)
        s_rope = sem("rope_steps", 3 * 4 * DEPTH, 1)
        s_vs = sem("shifted_v_loaded", 16 * 7 * DEPTH, 16)
        s_nml = sem("local_max_done", 8 * DEPTH)
        s_rl = sem("local_reciprocals", 8 * DEPTH)
        s_pl = sem("local_probs_scaled", 8 * DEPTH)
        s_hs = sem("h_shifted", DEPTH)
        s_sq2 = sem("centred_squares", DEPTH)
        s_rs = sem("mlp_rstd", DEPTH)
        s_tn = sem("mlp_norm_steps", 5 * DEPTH)
        s_mh = sem("mlp_high", DEPTH)
        s_va = sem("constants_set")
        s_store = sem("output_stored", 16, 16)

        taken_by = {"act": act_took, "dve": dve_took}

        def bank(step, k=0):
            return ring[FILL[step, k] % RING]

        def fill(step, k=0):
            return FILL[step, k] + 1

        def took(step, k=0):
            return taken_by[TOOK[FILL[step, k]][0]].sem

        def taken(count, step, k=0, passes_ago=0):
            who, n = TOOK[FILL[step, k]]
            return count(taken_by[who], n - passes_ago * TAKEN[who])

        def user_before(step, k=0):
            return taken_by[TOOK[(FILL[step, k] - RING) % CYCLE][0]].sem

        def free(count, step, k=0):
            m = FILL[step, k] - RING
            who, n = TOOK[m % CYCLE]
            return count(taken_by[who], n - (m < 0) * TAKEN[who])

        loads = [
            (ident[:], t["c_ident"]), (centre[:], t["c_centre"]),
            (identb[:], t["c_identb"]), (mask[:, :, :], t["c_mask"].rearrange("a p c -> p a c")),
            (stage[:, 0:128], t["WqT"]), (stage[:, 128:256], t["WkT"]), (stage[:, 256:384], t["WvT"]),
            (wo_full[:], t["WoT"]),
            (lng[:], t["ln_g"].rearrange("l p -> p l")), (lnb[:], t["ln_b"].rearrange("l p -> p l")),
            (b2[:], t["b2"].rearrange("l p -> p l")),
            (tab[:, 0, :, :, :, :].rearrange("p a b n d -> p (a b) n d"), t["c_rope"].rearrange("a (n p) d -> p a n d", p=P)),
            (tab[:, 1, :, :, :, :].rearrange("p a b n d -> p (a b) n d"), t["c_rope"].rearrange("a (n p) d -> p a n d", p=P)),
        ]
        for k, name in enumerate(("bq", "bk", "bv")):
            loads.append((bias3[:, k * E:(k + 1) * E], t[name].rearrange("(n e) -> n e", n=1).to_broadcast([P, E])))
        loads.append((bo[:], t["bo"].rearrange("(p n) -> p n", n=1)))
        for l in range(DEPTH):
            loads += [(stage2[l][:, 0:3 * INNER], t["wqkv"][l]),
                      (wo_local[:, l, :, :], t["wo"][l].rearrange("(n p) f -> p n f", p=P)),
                      (wd[:, l, 0:2, :], t["w2"][l, 0:256].rearrange("(n p) f -> p n f", p=P)),
                      (wd[0:HID - 256, l, 2, :], t["w2"][l, 256:HID])]
            for a in range(2):
                loads.append((stage3[:, (2 * l + a) * 384:(2 * l + a) * 384 + HID], t["w1"][l, :, a * HID:(a + 1) * HID]))
                loads.append((b1[:, l, a, 0:2], t["b1"][l, a * HID:a * HID + 256].rearrange("(n p) -> p n", p=P)))
                loads.append((b1[0:HID - 256, l, a, 2:3], t["b1"][l, a * HID + 256:(a + 1) * HID].rearrange("(p n) -> p n", n=1)))
            for k, name in enumerate(("q_scale", "k_scale")):
                row = t[name][l:l + 1, :]
                loads.append((scale_rows[:, l, 0, k, :], row.to_broadcast([P, LD])))
                loads.append((scale_rows[:, l, 1, k, 0:32], row[:, 32:64].to_broadcast([P, 32])))
                loads.append((scale_rows[:, l, 1, k, 32:64], row[:, 0:32].to_broadcast([P, 32])))
        LOADS = len(loads)

        def local_out(step, copy):
            l, d = step[1:]
            b, pair = d // 2, 2 * (d % 2)
            ps = bank(step)[:, :].rearrange("p (a w h i) -> p a w h i", a=2, w=2, h=2)
            dst = oTl[:, pair:pair + 2, b * P:(b + 1) * P].rearrange("p a (w i) -> p a w i", w=2)
            copy(dst[0:64], ps[0:64, :, :, 0, :])
            copy(dst[64:128], ps[64:128, :, :, 1, :]).then_inc(took(step), 1)

        block = ctx.enter_context(nc.Block())

        @block.sync
        def _(sp):
            sp.wait_ge(s_set.sem, 3)
            for dst, src in loads:
                sp.dma_start(dst, src, allow_slow_non_contiguous=True).then_inc(s_w.sem, 16)

            with sp.Fori(0, B) as i:
                count = Count(sp, i, [s_full, s_heads[0], s_store, act_took, dve_took])
                for step in STEPS:
                    kind = step[0]
                    if kind == "norm_x":
                        sp.wait_ge(took(step), taken(count, step, passes_ago=1))
                        sp.dma_start(xt[:, :, :], t["x"][bass.ds(i, 1)].rearrange("o (n p) e -> p (o n) e", p=P)).then_inc(s_x.sem, 16)
                        sp.wait_ge(s_store.sem, count(s_store, 0))
                        sp.dma_start(xr[:, :, :], t["x"][bass.ds(i, 1)].rearrange("o (n p) e -> p (o n) e", p=P)).then_inc(s_xr.sem, 16)
                    if kind == "values_full":
                        b = step[1]
                        sp.wait_ge(s_full.sem, count(s_full, 9 * b + 9))
                        sp.dma_start(scratch.rearrange("h t d -> t h d")[b * P:(b + 1) * P], ofs[:, b % 2, :, :]).then_inc(s_heads[b % 2].sem, 16)
                    if kind == "attn_load":
                        sp.wait_ge(s_heads[1].sem, count(s_heads[1], 16 * NB // 2))
                        sp.wait_ge(s_heads[0].sem, count(s_heads[0], 16 * NB // 2))
                        sp.dma_start(orow[:, :, :], scratch.rearrange("h (a t) d -> (h a) (t d)", t=E // D)
                                     .rearrange("(n p) e -> p n e", p=P)).then_inc(s_orow.sem, 16)
                    if kind == "project":
                        l, b = step[1:]
                        sp.wait_ge(took(step, 2), taken(count, step, 2))
                        sp.dma_start(vs[64:128, b, :], v[0:64, b, :]).then_inc(s_vs.sem, 16)
                        if b + 1 < NB:
                            sp.dma_start(vs[0:64, b + 1, :], v[64:128, b, :]).then_inc(s_vs.sem, 16)
                    if kind == "final":
                        sp.wait_ge(took(step), taken(count, step))
                        sp.dma_start(out[bass.ds(i, 1)].rearrange("o (n p) e -> p (o n) e", p=P), ob[:, :, :]).then_inc(s_store.sem, 16)
            sp.wait_ge(s_store.sem, s_store.ahead + 16 * B)

        @block.gpsimd
        def _(pool):
            nc.gpsimd.memset(half[:], -0.5).then_inc(s_va.sem, 1)
            nc.gpsimd.memset(ones[:], 1.0).then_inc(s_va.sem, 1)
            nc.gpsimd.memset(mean_of[:], 1.0 / E).then_inc(s_va.sem, 1)
            nc.gpsimd.memset(vs[:, 0, :], 0.0).then_inc(s_va.sem, 1)
            nc.gpsimd.memset(kT[:, :, 0:WIN], 0.0).then_inc(s_va.sem, 1)
            pool.wait_ge(s_va.sem, 5)
            with pool.Fori(0, B) as i:
                count = Count(pool, i, [s_rl, s_rope, s_rot, s_ssq, s_stats, act_took, dve_took])
                for step in STEPS:
                    kind = step[0]
                    if kind == "norm_x":
                        pool.wait_ge(s_stats.sem, count(s_stats, 4))
                        nc.gpsimd.tensor_tensor(rs4[:], ve4[:], half[:, 0:NB], ALU.pow).then_inc(s_rstd.sem, 1)
                    if kind == "rope":
                        n = step[1] * NB + step[2]
                        q = qk[:, n % 2, :]
                        qh3 = q.rearrange("p (h d) -> p h d", d=LD)
                        pool.wait_ge(s_rot.sem, count(s_rot, n + 1))
                        nc.gpsimd.tensor_tensor(q, q, t2[:], ALU.add).then_inc(s_rope.sem, 1)
                        pool.wait_ge(s_ssq.sem, count(s_ssq, 2 * n + 2))
                        nc.gpsimd.tensor_tensor(rn[:], ssq[:, 1, :], half[:, 0:1].to_broadcast([P, 16]), ALU.pow).then_inc(s_rope.sem, 1)
                        pool.wait_ge(s_rope.sem, count(s_rope, 3 * n + 2))
                        nc.gpsimd.tensor_tensor(qh3, qh3, rn[:, :, None].to_broadcast([P, 16, LD]), ALU.mult).then_inc(s_rope.sem, 1)
                    if kind == "scores":
                        n = step[1] * 8 + step[2]
                        pool.wait_ge(s_rl.sem, count(s_rl, n + 1))
                        pb = pl[:, n % 2, :, :]
                        nc.gpsimd.tensor_tensor(pb, pb, rl[:, n % 2, :, None].to_broadcast([P, HW, P]), ALU.mult).then_inc(s_pl.sem, 1)
                    if kind == "variance":
                        pool.wait_ge(took(step), taken(count, step))
                        nc.gpsimd.tensor_tensor(rsq[:], veps[:], half[:], ALU.pow).then_inc(s_rs.sem, 1)

        @block.scalar
        def _(act):
            act.wait_ge(s_w.sem, 16 * LOADS)
            with act.Fori(0, B) as i:
                count = Count(act, i, [s_full, s_nml, s_ssq, s_tn, s_vs, act_took, dve_took, filled])

                def copy(dst, src, **kw):
                    return nc.scalar.activation(dst, src, ACT.Copy, **kw)

                for step in STEPS:
                    kind = step[0]
                    if kind == "norm_x":
                        act.wait_ge(filled.sem, count(filled, fill(step)))
                        act.wait_ge(took(("attn_out",)), taken(count, ("attn_out",), passes_ago=1))
                        copy(xT[0][:], bank(step)[:]).then_inc(took(step), 1)
                        act.wait_ge(took(step), taken(count, step))
                        copy(xh[:], xT[0][:]).then_inc(s_xh.sem, 1)
                    if kind == "shift":
                        l = step[1]
                        src = xT[l]
                        if l == 0:
                            act.wait_ge(took(("norm_x",)), taken(count, ("norm_x",)))
                        else:
                            act.wait_ge(took(("down", l - 1)), taken(count, ("down", l - 1)))
                            act.wait_ge(filled.sem, count(filled, fill(("project", l - 1, NB - 1), 2)))
                        copy(hh[0:64, :], src[0:64, :])
                        copy(hh[64:128, 1:S], src[64:128, 0:S - 1]).then_inc(s_hh.sem, 1)
                    if kind == "project":
                        l, b = step[1:]
                        n = l * NB + b
                        for k in range(2):
                            act.wait_ge(filled.sem, count(filled, fill(step, k)))
                            if k == 0 and n >= 2:
                                act.wait_ge(filled.sem, count(filled, fill(("qk_t", (n - 2) // NB, (n - 2) % NB), 1)))
                            copy(qk[:, n % 2, k * 512:(k + 1) * 512], bank(step, k)[:]).then_inc(took(step, k), 1)
                        act.wait_ge(filled.sem, count(filled, fill(step, 2)))
                        if b == 0:
                            act.wait_ge(s_vs.sem, count(s_vs, 112 * l))
                        copy(v[:, b, :], bank(step, 2)[:]).then_inc(took(step, 2), 1)
                        act.wait_ge(took(step, 1), taken(count, step, 1))
                        act.wait_ge(s_ssq.sem, count(s_ssq, 2 * n))
                        nc.scalar.activation(sq[:], qk[:, n % 2, :], ACT.Square).then_inc(s_sq.sem, 1)
                    if kind == "qk_t":
                        l, b = step[1:]
                        act.wait_ge(filled.sem, count(filled, fill(step, 0)))
                        ps = bank(step, 0)[:, :].rearrange("p (a w i) -> p a w i", a=NPAIR, w=2)
                        if b >= 2:
                            act.wait_ge(filled.sem, count(filled, fill(("scores", l, 2 * (b - 2) + 1))))
                        copy(qbd[0:64, b % 2, :, :, 0, :], ps[0:64])
                        copy(qbd[64:128, b % 2, :, :, 1, :], ps[64:128]).then_inc(took(step, 0), 1)
                    if kind == "scores":
                        n = step[1] * 8 + step[2]
                        act.wait_ge(s_nml.sem, count(s_nml, n + 1))
                        if n >= 2:
                            act.wait_ge(filled.sem, count(filled, fill(("probs_t", (n - 2) // 8, (n - 2) % 8))))
                        for k in range(HW):
                            last = nc.scalar.activation(pl[:, n % 2, k, :], bank(step)[:, k * P:(k + 1) * P], ACT.Exp,
                                                        bias=nml[:, n % 2, k:k + 1], accum_out=suml[:, n % 2, k:k + 1])
                        last.then_inc(took(step), 1)
                    if kind == "probs_t" and taker(step, 0) == "act":
                        act.wait_ge(filled.sem, count(filled, fill(step)))
                        if step[2] >= 2:
                            act.wait_ge(filled.sem, count(filled, fill(("values", step[1], step[2] - 2))))
                        copy(pT[:, 0, :, :], bank(step)[:, :].rearrange("p (a b) -> p a b", a=HW)).then_inc(took(step), 1)
                    if kind == "values" and taker(step, 0) == "act":
                        act.wait_ge(filled.sem, count(filled, fill(step)))
                        local_out(step, copy)
                    if kind == "out_local":
                        act.wait_ge(took(step), taken(count, step))
                        copy(hs[0:64, :], x2[0:64, :])
                        copy(hs[64:128, 1:S], x2[64:128, 0:S - 1]).then_inc(s_hs.sem, 1)
                    if kind == "center":
                        act.wait_ge(filled.sem, count(filled, fill(step)))
                        copy(hc[:], bank(step)[:]).then_inc(took(step), 1)
                        act.wait_ge(took(step), taken(count, step))
                        nc.scalar.activation(sq2[:], hc[:], ACT.Square).then_inc(s_sq2.sem, 1)
                    if kind == "spread":
                        act.wait_ge(s_tn.sem, count(s_tn, 5 * step[1] + 4))
                        copy(mh[:], hc[:]).then_inc(s_mh.sem, 1)
                    if kind == "up":
                        l, c = step[1:]
                        act.wait_ge(filled.sem, count(filled, fill(step, 0)))
                        if c > 0:
                            act.wait_ge(took(("up", l, c - 1), 1), taken(count, ("up", l, c - 1), 1))
                        nc.scalar.activation(gate[:], bank(step, 0)[:], ACT.Gelu, bias=b1[:, l, 1, c:c + 1]).then_inc(took(step, 0), 1)
                    if kind == "scores_full":
                        act.wait_ge(s_full.sem, count(s_full, 9 * step[1] + 4))
                        nc.scalar.activation(ef[:, :, :], sf[:, :, :], ACT.Exp, scale=SCALE).then_inc(s_exp.sem, 1)
                    if kind == "attn_t":
                        act.wait_ge(filled.sem, count(filled, fill(step)))
                        copy(oT[:], bank(step)[:]).then_inc(took(step), 1)

        @block.vector
        def _(dve):
            nc.vector.memset(wd[:, :, :, :], 0.0).then_inc(s_set.sem, 1)
            nc.vector.memset(b1[:, :, :, :], 0.0).then_inc(s_set.sem, 1)
            nc.vector.memset(stage3, 0.0).then_inc(s_set.sem, 1)
            dve.wait_ge(s_w.sem, 16 * LOADS)
            n = 0
            for dsth, dstl, src in ((w3h[:], w3l[:], stage[:, 0:384]),
                                    (wqh[:, 0, :], wql[:, 0, :], stage2[0][:, 0:3 * INNER]),
                                    (wqh[:, 1, :], wql[:, 1, :], stage2[1][:, 0:3 * INNER]),
                                    (wuh[:, :, :, :], wul[:, :, :, :], stage3[:, 0:1536].rearrange("p (a b c) -> p a b c", a=2, b=2))):
                nc.vector.tensor_copy(dsth, src).then_inc(s_prep.sem, 1)
                n += 1
                dve.wait_ge(s_prep.sem, n)
                nc.vector.tensor_tensor(dstl, src, dsth.bitcast(F32), ALU.subtract).then_inc(s_prep.sem, 1)
                n += 1
            for l in range(DEPTH):
                for a in range(2):
                    for k in range(2):
                        nc.vector.tensor_tensor(tab[:, l, a, k, :, :], tab[:, l, a, k, :, :],
                                                scale_rows[:, l, a, k, None, :].to_broadcast([P, NB, LD]),
                                                ALU.mult).then_inc(s_prep.sem, 1)
                        n += 1
            dve.wait_ge(s_prep.sem, n)
            assert n == PREPS
            for part in (hh, hl):
                nc.vector.memset(part[64:128, 0:1].bitcast(F32), 0.0)
            nc.vector.memset(qbd[:, :, :, :, :, :], 0.0).then_inc(s_prep.sem, 1)
            dve.wait_ge(s_prep.sem, n + 1)
            nc.vector.memset(st[:, :, :], 0.0).then_inc(act_took.sem, act_took.ahead)
            nc.vector.memset(ve4[:], 0.0).then_inc(dve_took.sem, dve_took.ahead)
            nc.vector.memset(nmf[:], 0.0).then_inc(s_ssq.sem, s_ssq.ahead)
            nc.vector.memset(sumf[:], 0.0).then_inc(s_rope.sem, s_rope.ahead)
            nc.vector.memset(rf[:], 0.0).then_inc(s_vs.sem, s_vs.ahead)
            nc.vector.memset(mean[:], 0.0).then_inc(s_store.sem, s_store.ahead)

            with dve.Fori(0, B) as i:
                count = Count(dve, i, [s_exp, s_full, s_heads[0], s_hh, s_mh, s_pl, s_rope, s_rs, s_rstd, s_sin, s_sq, s_ssq, s_stats, s_x, s_xh, s_xr, act_took, dve_took, filled])

                def copy(dst, src):
                    return nc.vector.tensor_copy(dst, src)

                for step in STEPS:
                    kind = step[0]
                    if kind == "norm_x":
                        dve.wait_ge(s_x.sem, count(s_x, 16))
                        for b in range(NB):
                            last = nc.vector.bn_stats(st[:, b, :], xt[:, b, :])
                        last.then_inc(s_stats.sem, 1)
                        me, se, mo, so = (st[:, :, k] for k in (1, 2, 4, 5))
                        dve.wait_ge(s_stats.sem, count(s_stats, 1))
                        nc.vector.tensor_tensor(mv[:, 0, :], me, mo, ALU.add)
                        nc.vector.tensor_tensor(mv[:, 1, :], me, mo, ALU.subtract)
                        nc.vector.tensor_tensor(mv[:, 2, :], se, so, ALU.add).then_inc(s_stats.sem, 1)
                        dve.wait_ge(s_stats.sem, count(s_stats, 2))
                        nc.vector.tensor_scalar(mean[:], mv[:, 0, :], 0.5, None, ALU.mult)
                        nc.vector.tensor_tensor(mv[:, 1, :], mv[:, 1, :], mv[:, 1, :], ALU.mult)
                        nc.vector.tensor_scalar(mv[:, 2, :], mv[:, 2, :], 1.0 / E, EPS, ALU.mult, ALU.add).then_inc(s_stats.sem, 1)
                        dve.wait_ge(s_stats.sem, count(s_stats, 3))
                        nc.vector.scalar_tensor_tensor(ve4[:], mv[:, 1, :], 0.25, mv[:, 2, :], ALU.mult, ALU.add).then_inc(s_stats.sem, 1)
                        dve.wait_ge(s_rstd.sem, count(s_rstd, 1))
                        for b in range(NB):
                            last = nc.vector.tensor_scalar(xt[:, b, :], xt[:, b, :], mean[:, b:b + 1], rs4[:, b:b + 1],
                                                           ALU.subtract, ALU.mult)
                        last.then_inc(s_xn.sem, 1)
                        dve.wait_ge(s_xh.sem, count(s_xh, 1))
                        nc.vector.tensor_tensor(xl[:], xT[0][:], xh[:].bitcast(F32), ALU.subtract).then_inc(s_xl.sem, 1)
                    if kind == "shift":
                        l = step[1]
                        src = xT[l]
                        dve.wait_ge(s_hh.sem, count(s_hh, l + 1))
                        nc.vector.tensor_tensor(hl[0:64, :], src[0:64, :], hh[0:64, :].bitcast(F32), ALU.subtract)
                        nc.vector.tensor_tensor(hl[64:128, 1:S], src[64:128, 0:S - 1], hh[64:128, 1:S].bitcast(F32),
                                                ALU.subtract).then_inc(s_hl.sem, 1)
                    if kind == "qkv_full":
                        dve.wait_ge(filled.sem, count(filled, fill(step)))
                        nc.vector.tensor_tensor(qkvf[:, step[1], :, :, :].rearrange("p k h d -> p (k h d)"), bank(step)[:, 0:3 * E], bias3[:],
                                                ALU.add).then_inc(took(step), 1)
                    if kind == "scores_full":
                        b = step[1]
                        pr4 = pr[:].rearrange("p (q k d) -> p q k d", q=H, k=H)
                        q, k = (qkvf[:, b, n, :, :] for n in range(2))
                        if b == 0:
                            dve.wait_ge(took(("qkv_full", NB - 1)), taken(count, ("qkv_full", NB - 1)))
                        nc.vector.tensor_tensor(pr4, q[:, :, None, :].to_broadcast([P, H, H, D]), k[:, None, :, :].to_broadcast([P, H, H, D]),
                                                ALU.mult).then_inc(s_full.sem, 1)
                        dve.wait_ge(s_full.sem, count(s_full, 9 * b + 1))
                        nc.vector.reduce_sum(sf[:, :, :], pr4, AX_X).then_inc(s_full.sem, 1)
                        dve.wait_ge(s_full.sem, count(s_full, 9 * b + 2))
                        nc.vector.tensor_reduce(nmf[:], sf[:, :, :], AX_X, ALU.max, negate=True).then_inc(s_full.sem, 1)
                        dve.wait_ge(s_full.sem, count(s_full, 9 * b + 3))
                        nc.vector.tensor_tensor(sf[:, :, :], sf[:, :, :], nmf[:, :, None].to_broadcast([P, H, H]), ALU.add).then_inc(s_full.sem, 1)
                    if kind == "values_full":
                        b = step[1]
                        pr4 = pr[:].rearrange("p (q d k) -> p q d k", q=H, d=D)
                        vt = qkvf[:, b, 2, :, :].rearrange("p k d -> p d k")
                        dve.wait_ge(s_exp.sem, count(s_exp, b + 1))
                        nc.vector.tensor_tensor(pr4, ef[:, :, None, :].to_broadcast([P, H, D, H]), vt[:, None, :, :].to_broadcast([P, H, D, H]),
                                                ALU.mult).then_inc(s_full.sem, 1)
                        nc.vector.reduce_sum(sumf[:], ef[:, :, :], AX_X).then_inc(s_full.sem, 1)
                        dve.wait_ge(s_full.sem, count(s_full, 9 * b + 6))
                        nc.vector.reduce_sum(of[:, :, :], pr4, AX_X).then_inc(s_full.sem, 1)
                        nc.vector.reciprocal(rf[:], sumf[:]).then_inc(s_full.sem, 1)
                        dve.wait_ge(s_full.sem, count(s_full, 9 * b + 8))
                        if b >= 2:
                            dve.wait_ge(s_heads[b % 2].sem, count(s_heads[b % 2], 16))
                        nc.vector.tensor_tensor(ofs[:, b % 2, :, :], of[:, :, :], rf[:, :, None].to_broadcast([P, H, D]), ALU.mult).then_inc(s_full.sem, 1)
                    if kind == "rope":
                        l, b = step[1:]
                        n = l * NB + b
                        q4 = qk[:, n % 2, :].rearrange("p (a h d) -> p a h d", a=2, h=LH)
                        cos = tab[:, l, 0, :, b, None, :].to_broadcast([P, 2, LH, LD])
                        sin = tab[:, l, 1, :, b, None, :]
                        dve.wait_ge(s_sq.sem, count(s_sq, n + 1))
                        dve.wait_ge(s_rope.sem, count(s_rope, 3 * n))
                        nc.vector.reduce_sum(ssq[:, 0, :], sq[:].rearrange("p (h d) -> p h d", d=LD), AX_X).then_inc(s_ssq.sem, 1)
                        t24 = t2[:].rearrange("p (a h d) -> p a h d", a=2, h=LH)
                        for k in range(2):
                            o, s_ = 32 * k, 32 - 32 * k
                            last = nc.vector.tensor_tensor(t24[:, :, :, o:o + 32], q4[:, :, :, s_:s_ + 32],
                                                           sin[:, :, :, o:o + 32].to_broadcast([P, 2, LH, 32]), ALU.mult)
                        last.then_inc(s_sin.sem, 1)
                        dve.wait_ge(s_sin.sem, count(s_sin, n + 1))
                        nc.vector.tensor_tensor(q4, q4, cos, ALU.mult).then_inc(s_rot.sem, 1)
                        dve.wait_ge(s_ssq.sem, count(s_ssq, 2 * n + 1))
                        nc.vector.tensor_scalar(ssq[:, 1, :], ssq[:, 0, :], TINY, None, ALU.max).then_inc(s_ssq.sem, 1)
                    if kind == "qk_t":
                        l, b = step[1:]
                        dve.wait_ge(filled.sem, count(filled, fill(step, 1)))
                        copy(kT[:, :, WIN + P * b:WIN + P * b + P],
                             bank(step, 1)[:, :].rearrange("p (a c) -> p a c", a=NPAIR)).then_inc(took(step, 1), 1)
                    if kind == "scores":
                        n = step[1] * 8 + step[2]
                        dve.wait_ge(filled.sem, count(filled, fill(step)))
                        nc.vector.tensor_reduce(nml[:, n % 2, :], bank(step)[:, :].rearrange("p (a b) -> p a b", a=HW), AX_X,
                                                ALU.max, negate=True).then_inc(s_nml.sem, 1)
                    if kind == "probs_t" and taker(step, 0) == "dve":
                        dve.wait_ge(filled.sem, count(filled, fill(step)))
                        if step[2] >= 2:
                            dve.wait_ge(filled.sem, count(filled, fill(("values", step[1], step[2] - 2))))
                        copy(pT[:, 1, :, :], bank(step)[:, :].rearrange("p (a b) -> p a b", a=HW)).then_inc(took(step), 1)
                    if kind == "values" and taker(step, 0) == "dve":
                        dve.wait_ge(filled.sem, count(filled, fill(step)))
                        local_out(step, copy)
                    if kind == "out_local":
                        dve.wait_ge(filled.sem, count(filled, fill(step)))
                        nc.vector.memset(hs[64:128, 0:1], 0.0)
                        nc.vector.tensor_tensor(x2[:], bank(step)[:], xT[step[1]][:], ALU.add).then_inc(took(step), 1)
                    if kind == "variance":
                        l = step[1]
                        dve.wait_ge(filled.sem, count(filled, fill(step)))
                        nc.vector.tensor_scalar(veps[:], bank(step)[:, 0:NB], EPS, None, ALU.add).then_inc(took(step), 1)
                        dve.wait_ge(s_rs.sem, count(s_rs, l + 1))
                        for b in range(NB):
                            last = nc.vector.tensor_scalar(rs[:, b * P:(b + 1) * P], ident[:], rsq[:, b:b + 1], None, ALU.mult)
                        last.then_inc(s_tn.sem, 2)
                    if kind == "spread":
                        l = step[1]
                        dve.wait_ge(filled.sem, count(filled, fill(step)))
                        nc.vector.tensor_tensor(hc[:], hc[:], bank(step)[:], ALU.mult).then_inc(took(step), 1)
                        dve.wait_ge(took(step), taken(count, step))
                        nc.vector.tensor_scalar(hc[:], hc[:], lng[:, l:l + 1], lnb[:, l:l + 1], ALU.mult, ALU.add).then_inc(s_tn.sem, 2)
                        dve.wait_ge(s_mh.sem, count(s_mh, l + 1))
                        nc.vector.tensor_tensor(ml[:], hc[:], mh[:].bitcast(F32), ALU.subtract).then_inc(s_tn.sem, 1)
                    if kind == "up":
                        l, c = step[1:]
                        dve.wait_ge(filled.sem, count(filled, fill(step, 1)))
                        dve.wait_ge(took(step, 0), taken(count, step, 0))
                        nc.vector.scalar_tensor_tensor(hid[:, c, :], bank(step, 1)[:], b1[:, l, 0, c:c + 1], gate[:],
                                                       ALU.add, ALU.mult).then_inc(took(step, 1), 1)
                    if kind == "down":
                        l = step[1]
                        dve.wait_ge(filled.sem, count(filled, fill(step)))
                        nc.vector.scalar_tensor_tensor(xT[l + 1][:], bank(step)[:], b2[:, l:l + 1], x2[:],
                                                       ALU.add, ALU.add).then_inc(took(step), 1)
                    if kind == "attn_out":
                        dve.wait_ge(filled.sem, count(filled, fill(step)))
                        dve.wait_ge(took(("down", DEPTH - 1)), taken(count, ("down", DEPTH - 1)))
                        nc.vector.scalar_tensor_tensor(rT[:], bank(step)[:], bo[:], xT[DEPTH][:], ALU.add, ALU.add).then_inc(took(step), 1)
                    if kind == "final":
                        dve.wait_ge(filled.sem, count(filled, fill(step)))
                        dve.wait_ge(s_xr.sem, count(s_xr, 16))
                        nc.vector.tensor_tensor(ob[:, :, :], bank(step)[:, :].rearrange("p (n e) -> p n e", n=NB), xr[:, :, :],
                                                ALU.add).then_inc(took(step), 1)
                    if step in RECIP_AFTER:
                        n = RECIP_AFTER[step]
                        if n >= 2:
                            dve.wait_ge(s_pl.sem, count(s_pl, n - 1))
                        dve.wait_ge(took(("scores", n // 8, n % 8)), taken(count, ("scores", n // 8, n % 8)))
                        nc.vector.reciprocal(rl[:, n % 2, :], suml[:, n % 2, :]).then_inc(s_rl.sem, 1)

        @block.tensor
        def _(pe):
            pe.wait_ge(s_w.sem, 16 * LOADS)
            pe.wait_ge(s_prep.sem, PREPS + 1)
            pe.wait_ge(s_va.sem, 5)
            mm = nc.tensor.matmul

            with pe.Fori(0, B) as i:
                count = Count(pe, i, [s_hl, s_hs, s_orow, s_pl, s_rope, s_sq2, s_tn, s_vs, s_xl, s_xn, act_took, dve_took])

                def parts3(dst, ah, al, bh, bl):
                    mm(dst, ah, bh, start=True, stop=False)
                    mm(dst, ah, bl, start=False, stop=False)
                    return mm(dst, al, bh, start=False, stop=True)

                for step in STEPS:
                    kind = step[0]
                    if kind == "norm_x":
                        pe.wait_ge(user_before(step), free(count, step))
                        ps = bank(step)
                        pe.wait_ge(s_xn.sem, count(s_xn, 1))
                        for b in range(NB):
                            last = nc.tensor.transpose(ps[:, b * P:(b + 1) * P], xt[:, b, :], ident[:])
                        last.then_inc(filled.sem, 1)
                    if kind == "qkv_full":
                        pe.wait_ge(s_xl.sem, count(s_xl, 1))
                        c = slice(step[1] * P, (step[1] + 1) * P)
                        pe.wait_ge(user_before(step), free(count, step))
                        parts3(bank(step)[:, 0:3 * E], xh[:, c], xl[:, c], w3h[:], w3l[:]).then_inc(filled.sem, 1)
                    if kind == "project":
                        l, b = step[1:]
                        pe.wait_ge(s_hl.sem, count(s_hl, l + 1))
                        c = slice(b * P, (b + 1) * P)
                        for k in range(3):
                            o = slice(k * INNER, (k + 1) * INNER)
                            pe.wait_ge(user_before(step, k), free(count, step, k))
                            parts3(bank(step, k)[:], hh[:, c], hl[:, c], wqh[:, l, o], wql[:, l, o]).then_inc(filled.sem, 1)
                    if kind == "qk_t":
                        l, b = step[1:]
                        n = l * NB + b
                        pe.wait_ge(s_rope.sem, count(s_rope, 3 * n + 3))
                        for k in range(2):
                            pe.wait_ge(user_before(step, k), free(count, step, k))
                            ps = bank(step, k)
                            for a in range(NPAIR):
                                last = nc.tensor.transpose(ps[:, a * P:(a + 1) * P], qk[:, n % 2, k * 512 + a * P:k * 512 + (a + 1) * P], ident[:])
                            last.then_inc(filled.sem, 1)
                    if kind == "scores":
                        l, d = step[1:]
                        b = d // 2
                        pe.wait_ge(took(("qk_t", l, b), 0), taken(count, ("qk_t", l, b), 0))
                        pe.wait_ge(took(("qk_t", l, b), 1), taken(count, ("qk_t", l, b), 1))
                        pe.wait_ge(user_before(step), free(count, step))
                        ps = bank(step)
                        for k in range(4):
                            pair, wi = 2 * (d % 2) + k // 2, 2 * b + k % 2
                            o = ps[:, k * P:(k + 1) * P]
                            mm(o, qbd[:, b % 2, pair, k % 2, :, :].rearrange("p a b -> p (a b)"), kT[:, pair, WIN * wi:WIN * wi + P], start=True, stop=False)
                            last = mm(o, identb[:], mask[:, int(wi == 0), :], start=False, stop=True)
                        last.then_inc(filled.sem, 1)
                    if kind == "probs_t":
                        n = step[1] * 8 + step[2]
                        pe.wait_ge(s_pl.sem, count(s_pl, n + 1))
                        pe.wait_ge(user_before(step), free(count, step))
                        ps = bank(step)
                        for k in range(HW):
                            last = nc.tensor.transpose(ps[:, k * P:(k + 1) * P], pl[:, n % 2, k, :], ident[:])
                        last.then_inc(filled.sem, 1)
                    if kind == "values":
                        l, d = step[1:]
                        b = d // 2
                        pe.wait_ge(took(("probs_t", l, d)), taken(count, ("probs_t", l, d)))
                        if d == 0:
                            pe.wait_ge(s_vs.sem, count(s_vs, 112 * (l + 1)))
                        pe.wait_ge(user_before(step), free(count, step))
                        ps = bank(step)
                        for k in range(4):
                            pair = 2 * (d % 2) + k // 2
                            vals = v[:, b, :] if k % 2 else vs[:, b, :]
                            last = mm(ps[:, k * P:(k + 1) * P], vals[:, pair * P:(pair + 1) * P], pT[:, d % 2, k, :], start=True, stop=True)
                        last.then_inc(filled.sem, 1)
                    if kind == "out_local":
                        l = step[1]
                        pe.wait_ge(took(("values", l, 6)), taken(count, ("values", l, 6)))
                        pe.wait_ge(took(("values", l, 7)), taken(count, ("values", l, 7)))
                        pe.wait_ge(user_before(step), free(count, step))
                        ps = bank(step)
                        for a in range(NPAIR):
                            last = mm(ps[:], wo_local[:, l, a, :], oTl[:, a, :], start=a == 0, stop=a == NPAIR - 1)
                        last.then_inc(filled.sem, 1)
                    if kind == "center":
                        pe.wait_ge(s_hs.sem, count(s_hs, step[1] + 1))
                        pe.wait_ge(user_before(step), free(count, step))
                        mm(bank(step)[:], centre[:], hs[:], start=True, stop=True).then_inc(filled.sem, 1)
                    if kind == "variance":
                        pe.wait_ge(s_sq2.sem, count(s_sq2, step[1] + 1))
                        pe.wait_ge(user_before(step), free(count, step))
                        ps = bank(step)
                        for b in range(NB):
                            last = mm(ps[:, b:b + 1], sq2[:, b * P:(b + 1) * P], mean_of[:], start=True, stop=True)
                        last.then_inc(filled.sem, 1)
                    if kind == "spread":
                        pe.wait_ge(s_tn.sem, count(s_tn, 5 * step[1] + 2))
                        pe.wait_ge(user_before(step), free(count, step))
                        mm(bank(step)[:], ones[:], rs[:], start=True, stop=True).then_inc(filled.sem, 1)
                    if kind == "up":
                        l, c = step[1:]
                        if c == 0:
                            pe.wait_ge(s_tn.sem, count(s_tn, 5 * l + 5))
                        for k in range(2):
                            o = slice(c * P, (c + 1) * P)
                            pe.wait_ge(user_before(step, k), free(count, step, k))
                            parts3(bank(step, k)[:], wuh[:, l, 1 - k, o], wul[:, l, 1 - k, o], mh[:], ml[:]).then_inc(filled.sem, 1)
                    if kind == "down":
                        l = step[1]
                        pe.wait_ge(took(("up", l, HT - 1), 1), taken(count, ("up", l, HT - 1), 1))
                        pe.wait_ge(user_before(step), free(count, step))
                        ps = bank(step)
                        for c in range(HT):
                            last = mm(ps[:], wd[:, l, c, :], hid[:, c, :], start=c == 0, stop=c == HT - 1)
                        last.then_inc(filled.sem, 1)
                    if kind == "attn_t":
                        pe.wait_ge(s_orow.sem, count(s_orow, 16))
                        pe.wait_ge(user_before(step), free(count, step))
                        ps = bank(step)
                        for b in range(NB):
                            last = nc.tensor.transpose(ps[:, b * P:(b + 1) * P], orow[:, b, :], ident[:])
                        last.then_inc(filled.sem, 1)
                    if kind == "attn_out":
                        pe.wait_ge(took(("attn_t",)), taken(count, ("attn_t",)))
                        pe.wait_ge(user_before(step), free(count, step))
                        mm(bank(step)[:], wo_full[:], oT[:], start=True, stop=True).then_inc(filled.sem, 1)
                    if kind == "final":
                        pe.wait_ge(took(("attn_out",)), taken(count, ("attn_out",)))
                        pe.wait_ge(user_before(step), free(count, step))
                        ps = bank(step)
                        for b in range(NB):
                            last = nc.tensor.transpose(ps[:, b * P:(b + 1) * P], rT[:, b * P:(b + 1) * P], ident[:])
                        last.then_inc(filled.sem, 1)


def constants():
    import numpy as np

    f = np.float32
    i, c = np.arange(P)[:, None] % WIN, np.arange(P)[None, :]
    allowed = (i <= c) & (c <= i + WIN)
    masks = np.stack([np.where(allowed, 0.0, MASKED), np.where(allowed & (c >= WIN), 0.0, MASKED)])
    half_idx = np.arange(0, LD, 2, dtype=f)
    pos = np.arange(S, dtype=f)
    freqs = pos[:, None] * (f(1.0) / f(10000.0) ** (half_idx / f(LD)))[None, :]
    freqs = np.concatenate([freqs, freqs], axis=-1).astype(f)
    base = (half_idx + f(0.4 * LD)) / f(1.4 * LD)
    scale = base[None, :] ** ((pos - f(S // 2)) / f(WIN // 2))[:, None]
    scale = np.concatenate([scale, scale], axis=-1).astype(f)
    sign = np.where(np.arange(LD) < LD // 2, f(-1.0), f(1.0))
    cos, sin = np.cos(freqs), np.sin(freqs) * sign
    rope = np.stack([cos * scale * f(QK_SCALE), cos / scale, sin * scale * f(QK_SCALE), sin / scale])
    bf16 = mybir.dt.np(BF16)
    return {
        "c_ident": np.eye(P, dtype=f), "c_centre": (np.eye(P) - 1.0 / P).astype(f),
        "c_identb": np.eye(P).astype(bf16), "c_mask": masks.astype(bf16), "c_rope": rope.astype(f),
    }


def kernel(**inputs):
    import numpy as np
    from concourse import bacc
    from concourse.bass_utils import run_bass_kernel_spmd

    full, local = "L0_attn_", "L0_ffn_"
    arrays = {"x": inputs[full + "x"]}
    for name in ("Wq", "Wk", "Wv", "Wo"):
        arrays[name + "T"] = np.ascontiguousarray(np.asarray(inputs[full + name]).T)
    for name in ("bq", "bk", "bv", "bo"):
        arrays[name] = inputs[full + name]
    for name in ("wqkv", "q_scale", "k_scale", "wo", "ln_g", "ln_b", "w1", "b1", "w2", "b2"):
        arrays[name] = inputs[local + name]
    arrays = {k: np.ascontiguousarray(a) for k, a in arrays.items()} | constants()
    nc = bacc.Bacc("TRN2", target_bir_lowering=False, num_devices=1)
    t = {k: nc.dram_tensor(k, a.shape, mybir.dt.from_np(a.dtype), kind="ExternalInput").ap() for k, a in arrays.items()}
    out = nc.dram_tensor("out", (B, S, E), F32, kind="ExternalOutput").ap()
    build(nc, t, out)
    r = run_bass_kernel_spmd(nc, [arrays], core_ids=[0])
    return r.results[0]["out"]
```

```python
from contextlib import ExitStack

import concourse.bass as bass
from concourse import mybir

ALU = mybir.AluOpType
ACT = mybir.ActivationFunctionType
AX_X = mybir.AxisListType.X
F32 = mybir.dt.float32
F32R = mybir.dt.float32r
BF16 = mybir.dt.bfloat16

P = 128
B, S, E = 16, 512, 128
NB = S // P
H, D = 16, 8
DEPTH, LH, LD, WIN = 2, 8, 64, 64
INNER = LH * LD
NPAIR = LH // 2
NW = S // WIN
HW = NW // 2
HID = 341
HT = 3
QK_SCALE = 8.0
EPS = 1e-5
TINY = 1e-24
MASKED = -2.0 ** 124
RING = 8
SCALE = float(D) ** -0.5


PERIOD = 12
NU = 2 * DEPTH
EARLY = 12


def schedule():
    at = []
    for u in range(NU):
        unit = []
        for b in range(NB):
            unit += [(2 * b - 1, 6, ("project", u, b)), (2 * b, 5, ("rope", u, b)), (2 * b + 1, 4, ("qk_t", u, b))]
        for d in range(8):
            unit += [(d + 2, 3, ("scores", u, d)), (d + 3, 0, ("scale", u, d)), (d + 4, 2, ("probs_t", u, d)), (d + 6, 1, ("values", u, d))]
        unit += [(-2, 8, ("shift", u)), (14, 4, ("out_local", u)), (15, 7, ("center", u)), (16, 7, ("variance", u)),
                 (17, 7, ("spread", u)), (18, 7, ("up", u, 0)), (18, 7, ("up", u, 1)), (18, 7, ("up", u, 2)), (20, 4, ("down", u))]
        if u >= NU - 2:
            unit += [(14, 8, ("load_again", u % 2)), (18, 9, ("attn_t", u % 2)),
                     (21, 7, ("attn_out", u % 2)), (22, 7, ("final", u % 2))]
        at += [(slot + PERIOD * u, rank, step) for slot, rank, step in unit]
    for c in range(2):
        o = PERIOD * c
        at += [(o - 12, 8, ("load", c)), (o - 8, 8, ("norm_x", c)), (24 + 2 * o, 9, ("attn_load", c))]
        for b in range(NB):
            at += [(o + (-5, -4, -3, -1)[b], 7, ("qkv_full", c, b)), (2 * o + 6 * b, 9, ("scores_full", c, b)),
                   (2 * o + 6 * b + 3, 9, ("values_full", c, b))]
    at.sort(key=lambda e: e[:2])
    early = [step for slot, _, step in at if slot < EARLY]
    once = sorted([(slot + PERIOD * NU * (slot < EARLY), rank, step) for slot, rank, step in at], key=lambda e: e[:2])
    return early, [step for _, _, step in once]


def taker(step, k):
    kind = step[0]
    if kind in ("norm_x", "project", "center", "attn_t", "scores"):
        return "act"
    if kind in ("qk_t", "up"):
        return ("act", "dve")[k]
    if kind == "probs_t":
        return ("act", "dve")[step[2] % 2]
    if kind == "values":
        return ("dve", "act")[step[2] % 2]
    return "dve"


BANKS = {"norm_x": 1, "qkv_full": 1, "project": 3, "qk_t": 2, "scores": 1, "probs_t": 1, "values": 1, "out_local": 1,
         "center": 1, "variance": 1, "spread": 1, "up": 2, "down": 1, "attn_t": 1, "attn_out": 1, "final": 1}
PREPS = 8 + 4 * DEPTH


class Segment:

    def __init__(self, steps):
        self.steps = steps
        self.place = {step: n for n, step in enumerate(steps)}
        self.fills = [(step, k) for step in steps for k in range(BANKS.get(step[0], 0))]
        self.number = {fill: n for n, fill in enumerate(self.fills)}
        while len(self.fills) % RING:
            self.fills.append(self.fills[-RING])


BEFORE, PASS = [Segment(steps) for steps in schedule()]


class Signal:

    def __init__(self, sem, events, unit=1, ahead=0):
        self.sem, self.unit, self.ahead, self.number, self.total = sem, unit, ahead, {}, {}
        for segment in (BEFORE, PASS):
            n, number = 0, {}
            for step in segment.steps:
                if events(step):
                    number[step] = n
                    n += events(step)
            self.number[segment], self.total[segment] = number, unit * n
        self.first, self.per = ahead + self.total[BEFORE], self.total[PASS]


class Count:

    def __init__(self, segment, eng=None, i=None, signals=()):
        self.segment, self.base, self.step = segment, {}, None
        for signal in signals:
            if signal.per not in self.base:
                count = eng.alloc_register(f"{str(eng.engine).split('.')[-1]}_passes_times_{signal.per}")
                eng.reg_alu(count, i, signal.per, ALU.mult)
                self.base[signal.per] = eng.snap(count)

    def __call__(self, signal, step, m=1):
        place = self.segment.place
        if self.segment is BEFORE:
            if step not in place or place[step] > place[self.step]:
                assert signal.ahead > 0, (self.step, step)
                return signal.ahead
            return signal.ahead + signal.unit * (signal.number[BEFORE][step] + m)
        n = signal.first + signal.unit * (signal.number[PASS][step] + m)
        if place[step] > place[self.step]:
            n -= signal.per
        assert n > 0, (self.step, step)
        return self.base[signal.per] + n


def back(step, n, per_unit):
    kind, u, b = step
    u, b = divmod((u * per_unit + b - n) % (NU * per_unit), per_unit)
    return kind, u, b


def full_before(step, n):
    c, b = divmod((step[1] * NB + step[2] - n) % (2 * NB), NB)
    return "values_full", c, b


def build(nc, t, out):
    with ExitStack() as ctx:
        def sb(name, shape, dt=F32):
            return ctx.enter_context(nc.sbuf_tensor("sb_" + name, shape, dt))

        signals = []

        def signal(name, kinds, events=1, unit=1, ahead=0):
            count = events if callable(events) else (lambda step: events)
            s = Signal(ctx.enter_context(nc.semaphore(name)), lambda step: count(step) if step[0] in kinds else 0, unit, ahead)
            signals.append(s)
            return s

        w3h, w3l = sb("w3h", [P, 3 * E], F32R), sb("w3l", [P, 3 * E], F32R)
        wo_full = sb("wo_full", [P, E])
        wqh, wql = sb("wqh", [P, DEPTH, 3 * INNER], F32R), sb("wql", [P, DEPTH, 3 * INNER], F32R)
        wuh, wul = sb("wuh", [P, DEPTH, 2, HT * P], F32R), sb("wul", [P, DEPTH, 2, HT * P], F32R)
        wo_local = sb("wo_local", [P, DEPTH, NPAIR, E])
        wd = sb("wd", [P, DEPTH, HT, E])
        bias3 = sb("bias3", [P, 3 * E])
        bo = sb("bo", [P, 1])
        lng, lnb, b2 = sb("lng", [P, DEPTH]), sb("lnb", [P, DEPTH]), sb("b2", [P, DEPTH])
        b1 = sb("b1", [P, DEPTH, 2, HT])
        ident, centre = sb("ident", [P, P]), sb("centre", [P, P])
        ones, mean_of = sb("ones", [P, P]), sb("mean_of", [P, 1])
        identb, mask = sb("identb", [P, P], BF16), sb("mask", [P, 2, P], BF16)
        half = sb("half", [P, NB])
        tab = sb("tab", [P, DEPTH, 2, 2, NB, LD])

        xt = sb("xt", [P, 2, NB, E])
        st, mv, mean = sb("st", [P, NB, 6]), sb("mv", [P, 3, NB]), sb("mean", [P, NB])
        ve4, rs4 = sb("ve4", [P, NB]), sb("rs4", [P, NB])
        xT = [sb(f"xT{c}", [P, S]) for c in range(2)]
        xh, xl = sb("xh", [P, S], F32R), sb("xl", [P, S], F32R)
        qkvf = sb("qkvf", [P, 2, NB, 3, H, D])
        pr = sb("pr", [P, H * H * D])
        sf, ef = sb("sf", [P, H, H]), sb("ef", [P, H, H])
        nmf, sumf, rf = sb("nmf", [P, H]), sb("sumf", [P, H]), sb("rf", [P, H])
        of, ofs = sb("of", [P, H, D]), sb("ofs", [P, 2, H, D])
        orow, oT = sb("orow", [P, NB, E]), sb("oT", [P, S])
        hh, hl = sb("hh", [P, S], F32R), sb("hl", [P, S], F32R)
        qk, sq = sb("qk", [P, 2, 1024]), sb("sq", [P, 1024])
        ssq, rn = sb("ssq", [P, 2, 16]), sb("rn", [P, 16])
        t2 = sb("t2", [P, 1024])
        qbd = sb("qbd", [P, 2, NPAIR, 2, 2, WIN])
        kT = sb("kT", [P, NPAIR, WIN + S])
        v, vs = sb("v", [P, NB, INNER]), sb("vs", [P, NB, INNER])
        nml, suml, rl = sb("nml", [P, 2, HW]), sb("suml", [P, 2, HW]), sb("rl", [P, 2, HW])
        pl = sb("pl", [P, 2, HW, P])
        pT = sb("pT", [P, 2, HW, P])
        oTl = sb("oTl", [P, NPAIR, S])
        x2, hs, hc, rs, sq2 = [sb(name, [P, S]) for name in ("x2", "hs", "hc", "rs", "sq2")]
        veps, rsq = sb("veps", [P, NB]), sb("rsq", [P, NB])
        mh, ml = sb("mh", [P, S], F32R), sb("ml", [P, S], F32R)
        gate, hid = sb("gate", [P, S]), sb("hid", [P, HT, S])
        yT, rT, ob = sq2, hs, sb("ob", [P, NB, E])
        stage = pr[:]
        stage2 = [qk[:, :, :].rearrange("p a b -> p (a b)"), oTl[:, :, :].rearrange("p a b -> p (a b)")]
        stage3 = v[:, :, :].rearrange("p a b -> p (a b)")
        scale_rows = stage[:, 384:896].rearrange("p (l a k d) -> p l a k d", l=DEPTH, a=2, k=2)

        ring = [ctx.enter_context(nc.psum_tensor(f"ring{k}", [P, S], F32)) for k in range(RING)]
        scratch = nc.dram_tensor("heads_scratch", (H, S, D), F32, kind="Internal").ap()

        s_w = ctx.enter_context(nc.semaphore("weights_loaded"))
        s_set = ctx.enter_context(nc.semaphore("memory_set"))
        s_prep = ctx.enter_context(nc.semaphore("weights_split"))
        s_va = ctx.enter_context(nc.semaphore("constants_set"))
        s_x = [signal(f"x_loaded_{c}", ("load",), lambda step, c=c: step[1] == c, unit=16) for c in range(2)]
        s_xr = signal("x_again_loaded", ("load_again",), unit=16)
        s_store = signal("output_stored", ("final",), unit=16, ahead=16)
        s_stats = signal("stats_done", ("norm_x",), 4)
        s_rstd = signal("rstd_done", ("norm_x",))
        s_xn = signal("xn_done", ("norm_x",))
        s_xh = signal("x_high_done", ("norm_x",))
        s_xl = signal("x_low_done", ("norm_x",))
        s_fs = signal("full_scores_steps", ("scores_full",), 4)
        s_exp = signal("full_exponentials", ("scores_full",))
        s_fv = signal("full_values_steps", ("values_full",), 5, ahead=1)
        s_heads = [signal(f"heads_stored_{k}", ("values_full",), lambda step, k=k: step[2] % 2 == k, unit=16, ahead=16) for k in range(2)]
        s_orow = signal("heads_loaded", ("attn_load",), unit=16, ahead=32)
        s_hh = signal("h_high_done", ("shift",))
        s_hl = signal("h_low_done", ("shift",))
        s_sq = signal("squares_done", ("project",))
        s_sin = signal("sine_products", ("rope",))
        s_rot = signal("rotary_products", ("rope",))
        s_ssq = signal("square_sums", ("rope",), 2, ahead=1)
        s_rope = signal("rope_steps", ("rope",), 3, ahead=1)
        s_vs = [signal(f"shifted_v_loaded_{b}", ("project",), lambda step, b=b: int(step[2] in (b - 1, b)), unit=16)
                for b in range(NB)]
        s_nml = signal("local_max_done", ("scores",))
        s_rl = signal("local_reciprocals", ("scale",))
        s_pl = signal("local_probs_scaled", ("scale",), ahead=1)
        s_hs = signal("h_shifted", ("out_local",))
        s_sq2 = signal("centred_squares", ("center",))
        s_rs = signal("mlp_rstd", ("variance",))
        s_diag = signal("rstd_diagonals", ("variance",))
        s_tn = signal("mlp_norm_steps", ("spread",), 2)
        s_mh = signal("mlp_high", ("spread",))
        filled = signal("ring_filled", BANKS, lambda step: BANKS[step[0]])
        taken_by = {who: signal(f"{who}_took_bank", BANKS, lambda step, who=who: sum(taker(step, k) == who for k in range(BANKS[step[0]])))
                    for who in ("act", "dve")}
        for s in (filled, *taken_by.values()):
            s.ahead = s.per
            s.first += s.per

        def bank(count, step, k=0):
            return ring[count.segment.number[step, k] % RING]

        def took(step, k=0):
            return taken_by[taker(step, k)].sem

        def taken(count, step, k=0):
            who = taker(step, k)
            return count(taken_by[who], step, sum(taker(step, q) == who for q in range(k + 1)))

        def user_before(count, step, k=0):
            return count.segment.fills[(count.segment.number[step, k] - RING) % len(count.segment.fills)]

        def took_before(count, step, k=0):
            return took(*user_before(count, step, k))

        def free(count, step, k=0):
            return taken(count, *user_before(count, step, k))

        x_pairs = t["x"].rearrange("(j c) (n p) e -> j c p n e", c=2, p=P)
        out_pairs = out.rearrange("(j c) (n p) e -> j c p n e", c=2, p=P)

        loads = [
            (ident[:], t["c_ident"]), (centre[:], t["c_centre"]),
            (identb[:], t["c_identb"]), (mask[:, :, :], t["c_mask"].rearrange("a p c -> p a c")),
            (stage[:, 0:128], t["WqT"]), (stage[:, 128:256], t["WkT"]), (stage[:, 256:384], t["WvT"]),
            (wo_full[:], t["WoT"]),
            (lng[:], t["ln_g"].rearrange("l p -> p l")), (lnb[:], t["ln_b"].rearrange("l p -> p l")),
            (b2[:], t["b2"].rearrange("l p -> p l")),
            (tab[:, 0, :, :, :, :].rearrange("p a b n d -> p (a b) n d"), t["c_rope"].rearrange("a (n p) d -> p a n d", p=P)),
            (tab[:, 1, :, :, :, :].rearrange("p a b n d -> p (a b) n d"), t["c_rope"].rearrange("a (n p) d -> p a n d", p=P)),
        ]
        for k, name in enumerate(("bq", "bk", "bv")):
            loads.append((bias3[:, k * E:(k + 1) * E], t[name].rearrange("(n e) -> n e", n=1).to_broadcast([P, E])))
        loads.append((bo[:], t["bo"].rearrange("(p n) -> p n", n=1)))
        for l in range(DEPTH):
            loads += [(stage2[l][:, 0:3 * INNER], t["wqkv"][l]),
                      (wo_local[:, l, :, :], t["wo"][l].rearrange("(n p) f -> p n f", p=P)),
                      (wd[:, l, 0:2, :], t["w2"][l, 0:256].rearrange("(n p) f -> p n f", p=P)),
                      (wd[0:HID - 256, l, 2, :], t["w2"][l, 256:HID])]
            for a in range(2):
                loads.append((stage3[:, (2 * l + a) * 384:(2 * l + a) * 384 + HID], t["w1"][l, :, a * HID:(a + 1) * HID]))
                loads.append((b1[:, l, a, 0:2], t["b1"][l, a * HID:a * HID + 256].rearrange("(n p) -> p n", p=P)))
                loads.append((b1[0:HID - 256, l, a, 2:3], t["b1"][l, a * HID + 256:(a + 1) * HID].rearrange("(p n) -> p n", n=1)))
            for k, name in enumerate(("q_scale", "k_scale")):
                row = t[name][l:l + 1, :]
                loads.append((scale_rows[:, l, 0, k, :], row.to_broadcast([P, LD])))
                loads.append((scale_rows[:, l, 1, k, 0:32], row[:, 32:64].to_broadcast([P, 32])))
                loads.append((scale_rows[:, l, 1, k, 32:64], row[:, 0:32].to_broadcast([P, 32])))
        LOADS = len(loads)

        def local_out(count, step, copy):
            _, u, d = step
            b, pair = d // 2, 2 * (d % 2)
            ps = bank(count, step)[:, :].rearrange("p (a w h i) -> p a w h i", a=2, w=2, h=2)
            dst = oTl[:, pair:pair + 2, b * P:(b + 1) * P].rearrange("p a (w i) -> p a w i", w=2)
            copy(dst[0:64], ps[0:64, :, :, 0, :])
            copy(dst[64:128], ps[64:128, :, :, 1, :]).then_inc(took(step), 1)

        def all_done(eng):
            for s in signals:
                if s.first > s.ahead:
                    eng.wait_ge(s.sem, s.first)

        block = ctx.enter_context(nc.Block())

        @block.sync
        def _(sp):
            sp.wait_ge(s_set, 3)
            for dst, src in loads:
                sp.dma_start(dst, src, allow_slow_non_contiguous=True).then_inc(s_w, 16)

            def run(count, this, following):
                for step in count.segment.steps:
                    kind, count.step = step[0], step
                    if kind == "load":
                        c = step[1]
                        sp.wait_ge(filled.sem, count(filled, ("norm_x", c)))
                        sp.dma_start(xt[:, c, :, :], x_pairs[following, c:c + 1].rearrange("j c p n e -> p (j c n) e")).then_inc(s_x[c].sem, 16)
                    if kind == "load_again":
                        c = step[1]
                        sp.wait_ge(s_store.sem, count(s_store, ("final", 1 - c)))
                        sp.dma_start(ob[:, :, :], x_pairs[this, c:c + 1].rearrange("j c p n e -> p (j c n) e")).then_inc(s_xr.sem, 16)
                    if kind == "values_full":
                        _, c, b = step
                        sp.wait_ge(s_fv.sem, count(s_fv, step, 5))
                        sp.dma_start(scratch.rearrange("h t d -> t h d")[b * P:(b + 1) * P], ofs[:, b % 2, :, :]).then_inc(s_heads[b % 2].sem, 16)
                    if kind == "project":
                        _, u, b = step
                        sp.wait_ge(took(step, 2), taken(count, step, 2))
                        sp.dma_start(vs[64:128, b, :], v[0:64, b, :]).then_inc(s_vs[b].sem, 16)
                        if b + 1 < NB:
                            sp.wait_ge(filled.sem, count(filled, ("values", (u - 1) % NU, 2 * b + 3)))
                            sp.dma_start(vs[0:64, b + 1, :], v[64:128, b, :]).then_inc(s_vs[b + 1].sem, 16)
                    if kind == "final":
                        c = step[1]
                        sp.wait_ge(took(step), taken(count, step))
                        sp.dma_start(out_pairs[this, c:c + 1].rearrange("j c p n e -> p (j c n) e"), ob[:, :, :]).then_inc(s_store.sem, 16)

            sp.wait_ge(s_prep, PREPS + 1)
            run(Count(BEFORE), None, slice(0, 1))
            all_done(sp)
            with sp.Fori(0, B // 2) as i:
                wrapped = sp.alloc_register("following_pair")
                sp.reg_alu(wrapped, i, 1, ALU.add)
                sp.reg_alu(wrapped, wrapped, B // 2 - 1, ALU.bitwise_and)
                run(Count(PASS, sp, i, signals), bass.ds(i, 1), bass.ds(sp.snap(wrapped), 1))
            sp.wait_ge(s_store.sem, s_store.ahead + B // 2 * s_store.per)
            for s in s_heads:
                sp.wait_ge(s.sem, s.first + B // 2 * s.per)
            for s in s_vs:
                sp.wait_ge(s.sem, s.first + B // 2 * s.per)

        @block.gpsimd
        def _(pool):
            nc.gpsimd.memset(half[:], -0.5).then_inc(s_va, 1)
            nc.gpsimd.memset(ones[:], 1.0).then_inc(s_va, 1)
            nc.gpsimd.memset(mean_of[:], 1.0 / E).then_inc(s_va, 1)
            nc.gpsimd.memset(vs[:, 0, :], 0.0).then_inc(s_va, 1)
            nc.gpsimd.memset(kT[:, :, 0:WIN], 0.0).then_inc(s_va, 1)

            def run(count):
                for step in count.segment.steps:
                    kind, count.step = step[0], step
                    if kind == "norm_x":
                        pool.wait_ge(s_stats.sem, count(s_stats, step, 4))
                        nc.gpsimd.tensor_tensor(rs4[:], ve4[:], half[:], ALU.pow).then_inc(s_rstd.sem, 1)
                    if kind == "rope":
                        _, u, b = step
                        q = qk[:, b % 2, :]
                        qh3 = q.rearrange("p (h d) -> p h d", d=LD)
                        pool.wait_ge(s_rot.sem, count(s_rot, step))
                        nc.gpsimd.tensor_tensor(q, q, t2[:], ALU.add).then_inc(s_rope.sem, 1)
                        pool.wait_ge(s_ssq.sem, count(s_ssq, step, 2))
                        nc.gpsimd.tensor_tensor(rn[:], ssq[:, 1, :], half[:, 0:1].to_broadcast([P, 16]), ALU.pow).then_inc(s_rope.sem, 1)
                        pool.wait_ge(s_rope.sem, count(s_rope, step, 2))
                        nc.gpsimd.tensor_tensor(qh3, qh3, rn[:, :, None].to_broadcast([P, 16, LD]), ALU.mult).then_inc(s_rope.sem, 1)
                    if kind == "scale":
                        d = step[2]
                        pool.wait_ge(s_rl.sem, count(s_rl, step))
                        pb = pl[:, d % 2, :, :]
                        nc.gpsimd.tensor_tensor(pb, pb, rl[:, d % 2, :, None].to_broadcast([P, HW, P]), ALU.mult).then_inc(s_pl.sem, 1)
                    if kind == "variance":
                        pool.wait_ge(took(step), taken(count, step))
                        nc.gpsimd.tensor_tensor(rsq[:], veps[:], half[:], ALU.pow).then_inc(s_rs.sem, 1)

            pool.wait_ge(s_va, 5)
            run(Count(BEFORE))
            all_done(pool)
            with pool.Fori(0, B // 2) as i:
                run(Count(PASS, pool, i, signals))

        @block.scalar
        def _(act):
            def copy(dst, src):
                return nc.scalar.activation(dst, src, ACT.Copy)

            def run(count):
                for step in count.segment.steps:
                    kind, count.step = step[0], step
                    if kind == "norm_x":
                        c = step[1]
                        act.wait_ge(filled.sem, count(filled, step))
                        copy(xT[c][:], bank(count, step)[:]).then_inc(took(step), 1)
                        act.wait_ge(took(step), taken(count, step))
                        act.wait_ge(filled.sem, count(filled, ("qkv_full", 1 - c, NB - 1)))
                        copy(xh[:], xT[c][:]).then_inc(s_xh.sem, 1)
                    if kind == "shift":
                        u = step[1]
                        src = xT[u % 2]
                        if u < 2:
                            act.wait_ge(took(("norm_x", u)), taken(count, ("norm_x", u)))
                        else:
                            act.wait_ge(took(("down", u - 2)), taken(count, ("down", u - 2)))
                        act.wait_ge(filled.sem, count(filled, ("project", (u - 1) % NU, NB - 1), 3))
                        copy(hh[0:64, :], src[0:64, :])
                        copy(hh[64:128, 1:S], src[64:128, 0:S - 1]).then_inc(s_hh.sem, 1)
                    if kind == "project":
                        _, u, b = step
                        for k in range(2):
                            act.wait_ge(filled.sem, count(filled, step, k + 1))
                            if k == 0:
                                act.wait_ge(filled.sem, count(filled, ("qk_t",) + back(step, 2, NB)[1:], 2))
                            copy(qk[:, b % 2, k * 512:(k + 1) * 512], bank(count, step, k)[:]).then_inc(took(step, k), 1)
                        act.wait_ge(filled.sem, count(filled, step, 3))
                        act.wait_ge(filled.sem, count(filled, ("values", (u - 1) % NU, min(2 * b + 3, 7))))
                        copy(v[:, b, :], bank(count, step, 2)[:]).then_inc(took(step, 2), 1)
                        act.wait_ge(took(step, 1), taken(count, step, 1))
                        act.wait_ge(s_ssq.sem, count(s_ssq, ("rope",) + back(step, 1, NB)[1:], 1))
                        nc.scalar.activation(sq[:], qk[:, b % 2, :], ACT.Square).then_inc(s_sq.sem, 1)
                    if kind == "qk_t":
                        _, u, b = step
                        act.wait_ge(filled.sem, count(filled, step, 1))
                        ps = bank(count, step, 0)[:, :].rearrange("p (a w i) -> p a w i", a=NPAIR, w=2)
                        before = back(step, 2, NB)
                        act.wait_ge(filled.sem, count(filled, ("scores", before[1], 2 * before[2] + 1)))
                        copy(qbd[0:64, b % 2, :, :, 0, :], ps[0:64])
                        copy(qbd[64:128, b % 2, :, :, 1, :], ps[64:128]).then_inc(took(step, 0), 1)
                    if kind == "scores":
                        d = step[2]
                        act.wait_ge(s_nml.sem, count(s_nml, step))
                        act.wait_ge(filled.sem, count(filled, ("probs_t",) + back(step, 2, 8)[1:]))
                        for k in range(HW):
                            last = nc.scalar.activation(pl[:, d % 2, k, :], bank(count, step)[:, k * P:(k + 1) * P], ACT.Exp,
                                                        bias=nml[:, d % 2, k:k + 1], accum_out=suml[:, d % 2, k:k + 1])
                        last.then_inc(took(step), 1)
                    if kind == "probs_t" and taker(step, 0) == "act":
                        act.wait_ge(filled.sem, count(filled, step))
                        act.wait_ge(filled.sem, count(filled, ("values",) + back(step, 2, 8)[1:]))
                        copy(pT[:, 0, :, :], bank(count, step)[:, :].rearrange("p (a b) -> p a b", a=HW)).then_inc(took(step), 1)
                    if kind == "values" and taker(step, 0) == "act":
                        act.wait_ge(filled.sem, count(filled, step))
                        local_out(count, step, copy)
                    if kind == "out_local":
                        act.wait_ge(took(step), taken(count, step))
                        copy(hs[0:64, :], x2[0:64, :])
                        copy(hs[64:128, 1:S], x2[64:128, 0:S - 1]).then_inc(s_hs.sem, 1)
                    if kind == "center":
                        act.wait_ge(filled.sem, count(filled, step))
                        copy(hc[:], bank(count, step)[:]).then_inc(took(step), 1)
                        act.wait_ge(took(step), taken(count, step))
                        nc.scalar.activation(sq2[:], hc[:], ACT.Square).then_inc(s_sq2.sem, 1)
                    if kind == "spread":
                        act.wait_ge(s_tn.sem, count(s_tn, step, 1))
                        copy(mh[:], hc[:]).then_inc(s_mh.sem, 1)
                    if kind == "up":
                        _, u, c = step
                        act.wait_ge(filled.sem, count(filled, step, 1))
                        if c > 0:
                            act.wait_ge(took(("up", u, c - 1), 1), taken(count, ("up", u, c - 1), 1))
                        nc.scalar.activation(gate[:], bank(count, step, 0)[:], ACT.Gelu, bias=b1[:, u // 2, 1, c:c + 1]).then_inc(took(step, 0), 1)
                    if kind == "scores_full":
                        act.wait_ge(s_fs.sem, count(s_fs, step, 4))
                        nc.scalar.activation(ef[:, :, :], sf[:, :, :], ACT.Exp, scale=SCALE).then_inc(s_exp.sem, 1)
                    if kind == "attn_load":
                        c = step[1]
                        for k in range(2):
                            act.wait_ge(s_heads[k].sem, count(s_heads[k], ("values_full", c, NB - 2 + k)))
                        act.wait_ge(filled.sem, count(filled, ("attn_t", 1 - c)))
                        act.dma_start(orow[:, :, :], scratch.rearrange("h (a t) d -> (h a) (t d)", t=E // D)
                                     .rearrange("(n p) e -> p n e", p=P)).then_inc(s_orow.sem, 16)
                    if kind == "attn_t":
                        act.wait_ge(filled.sem, count(filled, step))
                        copy(oT[:], bank(count, step)[:]).then_inc(took(step), 1)

            act.wait_ge(s_w, 16 * LOADS)
            act.wait_ge(s_prep, PREPS + 1)
            run(Count(BEFORE))
            all_done(act)
            with act.Fori(0, B // 2) as i:
                run(Count(PASS, act, i, signals))

        @block.vector
        def _(dve):
            nc.vector.memset(wd[:, :, :, :], 0.0).then_inc(s_set, 1)
            nc.vector.memset(b1[:, :, :, :], 0.0).then_inc(s_set, 1)
            nc.vector.memset(stage3, 0.0).then_inc(s_set, 1)
            dve.wait_ge(s_w, 16 * LOADS)
            n = 0
            for dsth, dstl, src in ((w3h[:], w3l[:], stage[:, 0:384]),
                                    (wqh[:, 0, :], wql[:, 0, :], stage2[0][:, 0:3 * INNER]),
                                    (wqh[:, 1, :], wql[:, 1, :], stage2[1][:, 0:3 * INNER]),
                                    (wuh[:, :, :, :], wul[:, :, :, :], stage3[:, 0:1536].rearrange("p (a b c) -> p a b c", a=2, b=2))):
                nc.vector.tensor_copy(dsth, src).then_inc(s_prep, 1)
                n += 1
                dve.wait_ge(s_prep, n)
                nc.vector.tensor_tensor(dstl, src, dsth.bitcast(F32), ALU.subtract).then_inc(s_prep, 1)
                n += 1
            for l in range(DEPTH):
                for a in range(2):
                    for k in range(2):
                        nc.vector.tensor_tensor(tab[:, l, a, k, :, :], tab[:, l, a, k, :, :],
                                                scale_rows[:, l, a, k, None, :].to_broadcast([P, NB, LD]),
                                                ALU.mult).then_inc(s_prep, 1)
                        n += 1
            dve.wait_ge(s_prep, n)
            assert n == PREPS
            for part in (hh, hl):
                nc.vector.memset(part[64:128, 0:1].bitcast(F32), 0.0)
            for s in signals:
                if s.ahead:
                    nc.vector.memset(of[:, :, :], 0.0).then_inc(s.sem, s.ahead)
                    dve.wait_ge(s.sem, s.ahead)
            nc.vector.memset(qbd[:, :, :, :, :, :], 0.0).then_inc(s_prep, 1)
            dve.wait_ge(s_prep, n + 1)

            def copy(dst, src):
                return nc.vector.tensor_copy(dst, src)

            def run(count):
                for step in count.segment.steps:
                    kind, count.step = step[0], step
                    if kind == "norm_x":
                        c = step[1]
                        x = xt[:, c, :, :]
                        dve.wait_ge(s_x[c].sem, count(s_x[c], ("load", c)))
                        for b in range(NB):
                            last = nc.vector.bn_stats(st[:, b, :], x[:, b, :])
                        last.then_inc(s_stats.sem, 1)
                        me, se, mo, so = (st[:, :, k] for k in (1, 2, 4, 5))
                        dve.wait_ge(s_stats.sem, count(s_stats, step, 1))
                        nc.vector.tensor_tensor(mv[:, 0, :], me, mo, ALU.add)
                        nc.vector.tensor_tensor(mv[:, 1, :], me, mo, ALU.subtract)
                        nc.vector.tensor_tensor(mv[:, 2, :], se, so, ALU.add).then_inc(s_stats.sem, 1)
                        dve.wait_ge(s_stats.sem, count(s_stats, step, 2))
                        nc.vector.tensor_scalar(mean[:], mv[:, 0, :], 0.5, None, ALU.mult)
                        nc.vector.tensor_tensor(mv[:, 1, :], mv[:, 1, :], mv[:, 1, :], ALU.mult)
                        nc.vector.tensor_scalar(mv[:, 2, :], mv[:, 2, :], 1.0 / E, EPS, ALU.mult, ALU.add).then_inc(s_stats.sem, 1)
                        dve.wait_ge(s_stats.sem, count(s_stats, step, 3))
                        nc.vector.scalar_tensor_tensor(ve4[:], mv[:, 1, :], 0.25, mv[:, 2, :], ALU.mult, ALU.add).then_inc(s_stats.sem, 1)
                        dve.wait_ge(s_rstd.sem, count(s_rstd, step))
                        for b in range(NB):
                            last = nc.vector.tensor_scalar(x[:, b, :], x[:, b, :], mean[:, b:b + 1], rs4[:, b:b + 1],
                                                           ALU.subtract, ALU.mult)
                        last.then_inc(s_xn.sem, 1)
                        dve.wait_ge(s_xh.sem, count(s_xh, step))
                        nc.vector.tensor_tensor(xl[:], xT[c][:], xh[:].bitcast(F32), ALU.subtract).then_inc(s_xl.sem, 1)
                    if kind == "shift":
                        src = xT[step[1] % 2]
                        dve.wait_ge(s_hh.sem, count(s_hh, step))
                        nc.vector.tensor_tensor(hl[0:64, :], src[0:64, :], hh[0:64, :].bitcast(F32), ALU.subtract)
                        nc.vector.tensor_tensor(hl[64:128, 1:S], src[64:128, 0:S - 1], hh[64:128, 1:S].bitcast(F32),
                                                ALU.subtract).then_inc(s_hl.sem, 1)
                    if kind == "qkv_full":
                        _, c, b = step
                        dve.wait_ge(filled.sem, count(filled, step))
                        dve.wait_ge(s_fv.sem, count(s_fv, ("values_full", c, b), 5))
                        nc.vector.tensor_tensor(qkvf[:, c, b, :, :, :].rearrange("p k h d -> p (k h d)"), bank(count, step)[:, 0:3 * E],
                                                bias3[:], ALU.add).then_inc(took(step), 1)
                    if kind == "scores_full":
                        _, c, b = step
                        pr4 = pr[:].rearrange("p (q k d) -> p q k d", q=H, k=H)
                        q, k = (qkvf[:, c, b, n, :, :] for n in range(2))
                        dve.wait_ge(took(("qkv_full", c, b)), taken(count, ("qkv_full", c, b)))
                        dve.wait_ge(s_fv.sem, count(s_fv, full_before(step, 1), 5))
                        nc.vector.tensor_tensor(pr4, q[:, :, None, :].to_broadcast([P, H, H, D]), k[:, None, :, :].to_broadcast([P, H, H, D]),
                                                ALU.mult).then_inc(s_fs.sem, 1)
                        dve.wait_ge(s_fs.sem, count(s_fs, step, 1))
                        nc.vector.reduce_sum(sf[:, :, :], pr4, AX_X).then_inc(s_fs.sem, 1)
                        dve.wait_ge(s_fs.sem, count(s_fs, step, 2))
                        nc.vector.tensor_reduce(nmf[:], sf[:, :, :], AX_X, ALU.max, negate=True).then_inc(s_fs.sem, 1)
                        dve.wait_ge(s_fs.sem, count(s_fs, step, 3))
                        nc.vector.tensor_tensor(sf[:, :, :], sf[:, :, :], nmf[:, :, None].to_broadcast([P, H, H]), ALU.add).then_inc(s_fs.sem, 1)
                    if kind == "values_full":
                        _, c, b = step
                        pr4 = pr[:].rearrange("p (q d k) -> p q d k", q=H, d=D)
                        vt = qkvf[:, c, b, 2, :, :].rearrange("p k d -> p d k")
                        dve.wait_ge(s_exp.sem, count(s_exp, ("scores_full", c, b)))
                        nc.vector.tensor_tensor(pr4, ef[:, :, None, :].to_broadcast([P, H, D, H]), vt[:, None, :, :].to_broadcast([P, H, D, H]),
                                                ALU.mult).then_inc(s_fv.sem, 1)
                        nc.vector.reduce_sum(sumf[:], ef[:, :, :], AX_X).then_inc(s_fv.sem, 1)
                        dve.wait_ge(s_fv.sem, count(s_fv, step, 2))
                        nc.vector.reduce_sum(of[:, :, :], pr4, AX_X).then_inc(s_fv.sem, 1)
                        nc.vector.reciprocal(rf[:], sumf[:]).then_inc(s_fv.sem, 1)
                        dve.wait_ge(s_fv.sem, count(s_fv, step, 4))
                        if b == 0:
                            dve.wait_ge(s_orow.sem, count(s_orow, ("attn_load", 1 - c)))
                        dve.wait_ge(s_heads[b % 2].sem, count(s_heads[b % 2], full_before(step, 2)))
                        nc.vector.tensor_tensor(ofs[:, b % 2, :, :], of[:, :, :], rf[:, :, None].to_broadcast([P, H, D]), ALU.mult).then_inc(s_fv.sem, 1)
                    if kind == "rope":
                        _, u, b = step
                        q4 = qk[:, b % 2, :].rearrange("p (a h d) -> p a h d", a=2, h=LH)
                        cos = tab[:, u // 2, 0, :, b, None, :].to_broadcast([P, 2, LH, LD])
                        sin = tab[:, u // 2, 1, :, b, None, :]
                        dve.wait_ge(s_sq.sem, count(s_sq, ("project", u, b)))
                        dve.wait_ge(s_rope.sem, count(s_rope, back(step, 1, NB), 3))
                        nc.vector.reduce_sum(ssq[:, 0, :], sq[:].rearrange("p (h d) -> p h d", d=LD), AX_X).then_inc(s_ssq.sem, 1)
                        t24 = t2[:].rearrange("p (a h d) -> p a h d", a=2, h=LH)
                        for k in range(2):
                            o, s_ = 32 * k, 32 - 32 * k
                            last = nc.vector.tensor_tensor(t24[:, :, :, o:o + 32], q4[:, :, :, s_:s_ + 32],
                                                           sin[:, :, :, o:o + 32].to_broadcast([P, 2, LH, 32]), ALU.mult)
                        last.then_inc(s_sin.sem, 1)
                        dve.wait_ge(s_sin.sem, count(s_sin, step))
                        nc.vector.tensor_tensor(q4, q4, cos, ALU.mult).then_inc(s_rot.sem, 1)
                        dve.wait_ge(s_ssq.sem, count(s_ssq, step, 1))
                        nc.vector.tensor_scalar(ssq[:, 1, :], ssq[:, 0, :], TINY, None, ALU.max).then_inc(s_ssq.sem, 1)
                    if kind == "qk_t":
                        b = step[2]
                        dve.wait_ge(filled.sem, count(filled, step, 2))
                        copy(kT[:, :, WIN + P * b:WIN + P * b + P],
                             bank(count, step, 1)[:, :].rearrange("p (a c) -> p a c", a=NPAIR)).then_inc(took(step, 1), 1)
                    if kind == "scores":
                        d = step[2]
                        dve.wait_ge(filled.sem, count(filled, step))
                        nc.vector.tensor_reduce(nml[:, d % 2, :], bank(count, step)[:, :].rearrange("p (a b) -> p a b", a=HW), AX_X,
                                                ALU.max, negate=True).then_inc(s_nml.sem, 1)
                    if kind == "scale":
                        _, u, d = step
                        dve.wait_ge(s_pl.sem, count(s_pl, back(step, 2, 8)))
                        dve.wait_ge(took(("scores", u, d)), taken(count, ("scores", u, d)))
                        nc.vector.reciprocal(rl[:, d % 2, :], suml[:, d % 2, :]).then_inc(s_rl.sem, 1)
                    if kind == "probs_t" and taker(step, 0) == "dve":
                        dve.wait_ge(filled.sem, count(filled, step))
                        dve.wait_ge(filled.sem, count(filled, ("values",) + back(step, 2, 8)[1:]))
                        copy(pT[:, 1, :, :], bank(count, step)[:, :].rearrange("p (a b) -> p a b", a=HW)).then_inc(took(step), 1)
                    if kind == "values" and taker(step, 0) == "dve":
                        dve.wait_ge(filled.sem, count(filled, step))
                        local_out(count, step, copy)
                    if kind == "out_local":
                        u = step[1]
                        dve.wait_ge(filled.sem, count(filled, step))
                        nc.vector.memset(hs[64:128, 0:1], 0.0)
                        nc.vector.tensor_tensor(x2[:], bank(count, step)[:], xT[u % 2][:], ALU.add).then_inc(took(step), 1)
                    if kind == "variance":
                        dve.wait_ge(filled.sem, count(filled, step))
                        nc.vector.tensor_scalar(veps[:], bank(count, step)[:, 0:NB], EPS, None, ALU.add).then_inc(took(step), 1)
                        dve.wait_ge(s_rs.sem, count(s_rs, step))
                        for b in range(NB):
                            last = nc.vector.tensor_scalar(rs[:, b * P:(b + 1) * P], ident[:], rsq[:, b:b + 1], None, ALU.mult)
                        last.then_inc(s_diag.sem, 1)
                    if kind == "spread":
                        l = step[1] // 2
                        dve.wait_ge(filled.sem, count(filled, step))
                        nc.vector.tensor_tensor(hc[:], hc[:], bank(count, step)[:], ALU.mult).then_inc(took(step), 1)
                        dve.wait_ge(took(step), taken(count, step))
                        nc.vector.tensor_scalar(hc[:], hc[:], lng[:, l:l + 1], lnb[:, l:l + 1], ALU.mult, ALU.add).then_inc(s_tn.sem, 1)
                        dve.wait_ge(s_mh.sem, count(s_mh, step))
                        nc.vector.tensor_tensor(ml[:], hc[:], mh[:].bitcast(F32), ALU.subtract).then_inc(s_tn.sem, 1)
                    if kind == "up":
                        _, u, c = step
                        dve.wait_ge(filled.sem, count(filled, step, 2))
                        dve.wait_ge(took(step, 0), taken(count, step, 0))
                        nc.vector.scalar_tensor_tensor(hid[:, c, :], bank(count, step, 1)[:], b1[:, u // 2, 0, c:c + 1], gate[:],
                                                       ALU.add, ALU.mult).then_inc(took(step, 1), 1)
                    if kind == "down":
                        u = step[1]
                        to = yT if u >= NU - 2 else xT[u % 2]
                        dve.wait_ge(filled.sem, count(filled, step))
                        nc.vector.scalar_tensor_tensor(to[:], bank(count, step)[:], b2[:, u // 2:u // 2 + 1], x2[:],
                                                       ALU.add, ALU.add).then_inc(took(step), 1)
                    if kind == "attn_out":
                        down = ("down", NU - 2 + step[1])
                        dve.wait_ge(filled.sem, count(filled, step))
                        dve.wait_ge(took(down), taken(count, down))
                        nc.vector.scalar_tensor_tensor(rT[:], bank(count, step)[:], bo[:], yT[:], ALU.add, ALU.add).then_inc(took(step), 1)
                    if kind == "final":
                        dve.wait_ge(filled.sem, count(filled, step))
                        dve.wait_ge(s_xr.sem, count(s_xr, ("load_again", step[1])))
                        nc.vector.tensor_tensor(ob[:, :, :], bank(count, step)[:, :].rearrange("p (n e) -> p n e", n=NB), ob[:, :, :],
                                                ALU.add).then_inc(took(step), 1)

            run(Count(BEFORE))
            all_done(dve)
            with dve.Fori(0, B // 2) as i:
                run(Count(PASS, dve, i, signals))

        @block.tensor
        def _(pe):
            mm = nc.tensor.matmul

            def parts3(dst, ah, al, bh, bl):
                mm(dst, ah, bh, start=True, stop=False)
                mm(dst, ah, bl, start=False, stop=False)
                return mm(dst, al, bh, start=False, stop=True)

            def run(count):
                def claim(step, k=0):
                    return took_before(count, step, k), free(count, step, k)

                for step in count.segment.steps:
                    kind, count.step = step[0], step
                    ps = bank(count, step) if kind in BANKS else None
                    if kind == "norm_x":
                        c = step[1]
                        pe.wait_ge(*claim(step))
                        pe.wait_ge(s_xn.sem, count(s_xn, step))
                        for b in range(NB):
                            last = nc.tensor.transpose(ps[:, b * P:(b + 1) * P], xt[:, c, b, :], ident[:])
                        last.then_inc(filled.sem, 1)
                    if kind == "qkv_full":
                        _, c, b = step
                        pe.wait_ge(*claim(step))
                        pe.wait_ge(s_xl.sem, count(s_xl, ("norm_x", c)))
                        o = slice(b * P, (b + 1) * P)
                        parts3(ps[:, 0:3 * E], xh[:, o], xl[:, o], w3h[:], w3l[:]).then_inc(filled.sem, 1)
                    if kind == "project":
                        _, u, b = step
                        pe.wait_ge(s_hl.sem, count(s_hl, ("shift", u)))
                        c = slice(b * P, (b + 1) * P)
                        for k in range(3):
                            o = slice(k * INNER, (k + 1) * INNER)
                            pe.wait_ge(*claim(step, k))
                            parts3(bank(count, step, k)[:], hh[:, c], hl[:, c], wqh[:, u // 2, o], wql[:, u // 2, o]).then_inc(filled.sem, 1)
                    if kind == "qk_t":
                        _, u, b = step
                        pe.wait_ge(s_rope.sem, count(s_rope, ("rope", u, b), 3))
                        for k in range(2):
                            pe.wait_ge(*claim(step, k))
                            ps = bank(count, step, k)
                            for a in range(NPAIR):
                                last = nc.tensor.transpose(ps[:, a * P:(a + 1) * P], qk[:, b % 2, k * 512 + a * P:k * 512 + (a + 1) * P], ident[:])
                            last.then_inc(filled.sem, 1)
                    if kind == "scores":
                        _, u, d = step
                        b = d // 2
                        for k in range(2):
                            pe.wait_ge(took(("qk_t", u, b), k), taken(count, ("qk_t", u, b), k))
                        pe.wait_ge(*claim(step))
                        for k in range(4):
                            pair, wi = 2 * (d % 2) + k // 2, 2 * b + k % 2
                            o = ps[:, k * P:(k + 1) * P]
                            mm(o, qbd[:, b % 2, pair, k % 2, :, :].rearrange("p a b -> p (a b)"), kT[:, pair, WIN * wi:WIN * wi + P], start=True, stop=False)
                            last = mm(o, identb[:], mask[:, int(wi == 0), :], start=False, stop=True)
                        last.then_inc(filled.sem, 1)
                    if kind == "probs_t":
                        _, u, d = step
                        pe.wait_ge(s_pl.sem, count(s_pl, ("scale", u, d)))
                        pe.wait_ge(*claim(step))
                        for k in range(HW):
                            last = nc.tensor.transpose(ps[:, k * P:(k + 1) * P], pl[:, d % 2, k, :], ident[:])
                        last.then_inc(filled.sem, 1)
                    if kind == "values":
                        _, u, d = step
                        b = d // 2
                        pe.wait_ge(took(("probs_t", u, d)), taken(count, ("probs_t", u, d)))
                        if d % 2 == 0:
                            pe.wait_ge(s_vs[b].sem, count(s_vs[b], ("project", u, b)))
                        pe.wait_ge(*claim(step))
                        for k in range(4):
                            pair = 2 * (d % 2) + k // 2
                            vals = v[:, b, :] if k % 2 else vs[:, b, :]
                            last = mm(ps[:, k * P:(k + 1) * P], vals[:, pair * P:(pair + 1) * P], pT[:, d % 2, k, :], start=True, stop=True)
                        last.then_inc(filled.sem, 1)
                    if kind == "out_local":
                        u = step[1]
                        for d in (6, 7):
                            pe.wait_ge(took(("values", u, d)), taken(count, ("values", u, d)))
                        pe.wait_ge(*claim(step))
                        for a in range(NPAIR):
                            last = mm(ps[:], wo_local[:, u // 2, a, :], oTl[:, a, :], start=a == 0, stop=a == NPAIR - 1)
                        last.then_inc(filled.sem, 1)
                    if kind == "center":
                        pe.wait_ge(s_hs.sem, count(s_hs, ("out_local", step[1])))
                        pe.wait_ge(*claim(step))
                        mm(ps[:], centre[:], hs[:], start=True, stop=True).then_inc(filled.sem, 1)
                    if kind == "variance":
                        pe.wait_ge(s_sq2.sem, count(s_sq2, ("center", step[1])))
                        pe.wait_ge(*claim(step))
                        for b in range(NB):
                            last = mm(ps[:, b:b + 1], sq2[:, b * P:(b + 1) * P], mean_of[:], start=True, stop=True)
                        last.then_inc(filled.sem, 1)
                    if kind == "spread":
                        pe.wait_ge(s_diag.sem, count(s_diag, ("variance", step[1])))
                        pe.wait_ge(*claim(step))
                        mm(ps[:], ones[:], rs[:], start=True, stop=True).then_inc(filled.sem, 1)
                    if kind == "up":
                        _, u, c = step
                        if c == 0:
                            pe.wait_ge(s_tn.sem, count(s_tn, ("spread", u), 2))
                        for k in range(2):
                            o = slice(c * P, (c + 1) * P)
                            pe.wait_ge(*claim(step, k))
                            parts3(bank(count, step, k)[:], wuh[:, u // 2, 1 - k, o], wul[:, u // 2, 1 - k, o], mh[:], ml[:]).then_inc(filled.sem, 1)
                    if kind == "down":
                        u = step[1]
                        pe.wait_ge(took(("up", u, HT - 1), 1), taken(count, ("up", u, HT - 1), 1))
                        pe.wait_ge(*claim(step))
                        for c in range(HT):
                            last = mm(ps[:], wd[:, u // 2, c, :], hid[:, c, :], start=c == 0, stop=c == HT - 1)
                        last.then_inc(filled.sem, 1)
                    if kind == "attn_t":
                        pe.wait_ge(s_orow.sem, count(s_orow, ("attn_load", step[1])))
                        pe.wait_ge(*claim(step))
                        for b in range(NB):
                            last = nc.tensor.transpose(ps[:, b * P:(b + 1) * P], orow[:, b, :], ident[:])
                        last.then_inc(filled.sem, 1)
                    if kind == "attn_out":
                        pe.wait_ge(took(("attn_t", step[1])), taken(count, ("attn_t", step[1])))
                        pe.wait_ge(*claim(step))
                        mm(ps[:], wo_full[:], oT[:], start=True, stop=True).then_inc(filled.sem, 1)
                    if kind == "final":
                        pe.wait_ge(took(("attn_out", step[1])), taken(count, ("attn_out", step[1])))
                        pe.wait_ge(*claim(step))
                        for b in range(NB):
                            last = nc.tensor.transpose(ps[:, b * P:(b + 1) * P], rT[:, b * P:(b + 1) * P], ident[:])
                        last.then_inc(filled.sem, 1)

            pe.wait_ge(s_w, 16 * LOADS)
            pe.wait_ge(s_prep, PREPS + 1)
            pe.wait_ge(s_va, 5)
            run(Count(BEFORE))
            all_done(pe)
            with pe.Fori(0, B // 2) as i:
                run(Count(PASS, pe, i, signals))


def constants():
    import numpy as np

    f = np.float32
    i, c = np.arange(P)[:, None] % WIN, np.arange(P)[None, :]
    allowed = (i <= c) & (c <= i + WIN)
    masks = np.stack([np.where(allowed, 0.0, MASKED), np.where(allowed & (c >= WIN), 0.0, MASKED)])
    half_idx = np.arange(0, LD, 2, dtype=f)
    pos = np.arange(S, dtype=f)
    freqs = pos[:, None] * (f(1.0) / f(10000.0) ** (half_idx / f(LD)))[None, :]
    freqs = np.concatenate([freqs, freqs], axis=-1).astype(f)
    base = (half_idx + f(0.4 * LD)) / f(1.4 * LD)
    scale = base[None, :] ** ((pos - f(S // 2)) / f(WIN // 2))[:, None]
    scale = np.concatenate([scale, scale], axis=-1).astype(f)
    sign = np.where(np.arange(LD) < LD // 2, f(-1.0), f(1.0))
    cos, sin = np.cos(freqs), np.sin(freqs) * sign
    rope = np.stack([cos * scale * f(QK_SCALE), cos / scale, sin * scale * f(QK_SCALE), sin / scale])
    bf16 = mybir.dt.np(BF16)
    return {
        "c_ident": np.eye(P, dtype=f), "c_centre": (np.eye(P) - 1.0 / P).astype(f),
        "c_identb": np.eye(P).astype(bf16), "c_mask": masks.astype(bf16), "c_rope": rope.astype(f),
    }


def kernel(**inputs):
    import numpy as np
    from concourse import bacc
    from concourse.bass_utils import run_bass_kernel_spmd

    full, local = "L0_attn_", "L0_ffn_"
    arrays = {"x": inputs[full + "x"]}
    for name in ("Wq", "Wk", "Wv", "Wo"):
        arrays[name + "T"] = np.ascontiguousarray(np.asarray(inputs[full + name]).T)
    for name in ("bq", "bk", "bv", "bo"):
        arrays[name] = inputs[full + name]
    for name in ("wqkv", "q_scale", "k_scale", "wo", "ln_g", "ln_b", "w1", "b1", "w2", "b2"):
        arrays[name] = inputs[local + name]
    arrays = {k: np.ascontiguousarray(a) for k, a in arrays.items()} | constants()
    nc = bacc.Bacc("TRN2", target_bir_lowering=False, num_devices=1)
    t = {k: nc.dram_tensor(k, a.shape, mybir.dt.from_np(a.dtype), kind="ExternalInput").ap() for k, a in arrays.items()}
    out = nc.dram_tensor("out", (B, S, E), F32, kind="ExternalOutput").ap()
    build(nc, t, out)
    r = run_bass_kernel_spmd(nc, [arrays], core_ids=[0])
    return r.results[0]["out"]
```

```python
from contextlib import ExitStack

import concourse.bass as bass
from concourse import mybir

ALU = mybir.AluOpType
ACT = mybir.ActivationFunctionType
AX_X = mybir.AxisListType.X
F32 = mybir.dt.float32
F32R = mybir.dt.float32r
BF16 = mybir.dt.bfloat16

P = 128
B, S, E = 16, 512, 128
NB = S // P
H, D = 16, 8
DEPTH, LH, LD, WIN = 2, 8, 64, 64
INNER = LH * LD
NPAIR = LH // 2
NW = S // WIN
HW = NW // 2
HID = 341
HT = 3
QK_SCALE = 8.0
EPS = 1e-5
TINY = 1e-24
MASKED = -2.0 ** 124
RING = 8
SCALE = float(D) ** -0.5

PERIOD = 12
NU = 2 * DEPTH
EARLY = 12

UNIT_SLOTS = {
    "shift": (-3.122,), "project": (-1.844, -0.689, 1.878, 3.997), "rope": (-1.783, -0.068, 3.185, 4.640),
    "qk_t": (0.718, 3.346, 5.684, 6.239), "scores": (2.078, 2.179, 4.015, 4.961, 6.722, 6.889, 7.432, 8.303),
    "scale": (3.897, 4.233, 5.688, 6.171, 7.631, 8.717, 9.554, 9.592),
    "probs_t": (4.484, 4.707, 7.164, 7.895, 10.513, 10.590, 10.949, 12.388),
    "values": (4.796, 5.910, 9.040, 9.303, 10.824, 11.303, 12.634, 12.920), "out_local": (15.332,), "center": (15.531,),
    "variance": (16.401,), "diagonal": (16.851,), "spread": (17.308,), "up": (18.076, 18.207, 18.270), "down": (20.541,),
}
FIRST_SLOTS = {
    "load": (-10.257,),
    "norm_x": (-6.094,),
    "norm_t": (-5.564,),
    "qkv_full": (-4.380, -2.207, -1.542, 2.368),
}
FULL_SLOTS = {
    "product_full": (-0.934, 6.875, 11.558, 18.098),
    "scores_full": (1.770, 7.936, 13.730, 19.253),
    "exp_full": (2.774, 9.308, 15.100, 21.523),
    "values_full": (3.931, 11.264, 15.676, 22.654),
    "attn_load": (27.101,),
}
LAST_SLOTS = {
    "load_again": (14.384,),
    "attn_t": (17.883,),
    "attn_out": (21.447,),
    "final": (22.718,),
}


def slots():
    at = []
    for u in range(NU):
        at += [(PERIOD * u + slot, (kind, u, n)) for kind, all_n in UNIT_SLOTS.items() for n, slot in enumerate(all_n)]
    for c in range(2):
        for table, start in ((FIRST_SLOTS, PERIOD * c), (FULL_SLOTS, 2 * PERIOD * c), (LAST_SLOTS, PERIOD * (NU - 2 + c))):
            at += [(start + slot, (kind, c, n)) for kind, all_n in table.items() for n, slot in enumerate(all_n)]
    single = {kind for table in (UNIT_SLOTS, FIRST_SLOTS, FULL_SLOTS, LAST_SLOTS) for kind, all_n in table.items() if len(all_n) == 1}
    return [(slot, step[:2] if step[0] in single else step) for slot, step in at]


def schedule():
    at = slots()
    before = sorted((slot, step) for slot, step in at if slot < EARLY)
    a_pass = sorted((slot + PERIOD * NU * (slot < EARLY), step) for slot, step in at)
    return [step for _, step in before], [step for _, step in a_pass]


def taker(step, k):
    kind = step[0]
    if kind in ("norm_t", "project", "center", "attn_t", "scores", "probs_t", "values"):
        return "act"
    if kind in ("qk_t", "up"):
        return ("act", "dve")[k]
    return "dve"


BANKS = {"norm_t": 1, "qkv_full": 1, "project": 3, "qk_t": 2, "scores": 1, "probs_t": 1, "values": 1, "out_local": 1,
         "center": 1, "variance": 1, "spread": 1, "up": 2, "down": 1, "attn_t": 1, "attn_out": 1, "final": 1}
PREPS = 8 + 4 * DEPTH


class Segment:

    def __init__(self, steps):
        self.steps = steps
        self.place = {step: n for n, step in enumerate(steps)}
        self.fills = [(step, k) for step in steps for k in range(BANKS.get(step[0], 0))]
        self.number = {fill: n for n, fill in enumerate(self.fills)}
        while len(self.fills) % RING:
            self.fills.append(self.fills[-RING])


BEFORE, PASS = [Segment(steps) for steps in schedule()]


class Signal:

    def __init__(self, sem, events, unit=1, ahead=0):
        self.sem, self.unit, self.ahead, self.number, self.total = sem, unit, ahead, {}, {}
        for segment in (BEFORE, PASS):
            n, number = 0, {}
            for step in segment.steps:
                if events(step):
                    number[step] = n
                    n += events(step)
            self.number[segment], self.total[segment] = number, unit * n
        self.first, self.per = ahead + self.total[BEFORE], self.total[PASS]


class Count:

    def __init__(self, segment, eng=None, i=None, signals=()):
        self.segment, self.base, self.step = segment, {}, None
        for signal in signals:
            if signal.per not in self.base:
                count = eng.alloc_register(f"{str(eng.engine).split('.')[-1]}_passes_times_{signal.per}")
                eng.reg_alu(count, i, signal.per, ALU.mult)
                self.base[signal.per] = eng.snap(count)

    def __call__(self, signal, step, m=1):
        place = self.segment.place
        if self.segment is BEFORE:
            if step not in place or place[step] > place[self.step]:
                assert signal.ahead > 0, (self.step, step)
                return signal.ahead
            return signal.ahead + signal.unit * (signal.number[BEFORE][step] + m)
        n = signal.first + signal.unit * (signal.number[PASS][step] + m)
        if place[step] > place[self.step]:
            n -= signal.per
        assert n > 0, (self.step, step)
        return self.base[signal.per] + n


def back(step, n, per_unit):
    kind, u, b = step
    u, b = divmod((u * per_unit + b - n) % (NU * per_unit), per_unit)
    return kind, u, b


def full_before(step, n):
    c, b = divmod((step[1] * NB + step[2] - n) % (2 * NB), NB)
    return "values_full", c, b


def build(nc, t, out):
    with ExitStack() as ctx:
        def sb(name, shape, dt=F32):
            return ctx.enter_context(nc.sbuf_tensor("sb_" + name, shape, dt))

        signals = []

        def signal(name, kinds, events=1, unit=1, ahead=0):
            count = events if callable(events) else (lambda step: events)
            s = Signal(ctx.enter_context(nc.semaphore(name)), lambda step: count(step) if step[0] in kinds else 0, unit, ahead)
            signals.append(s)
            return s

        w3h, w3l = sb("w3h", [P, 3 * E], F32R), sb("w3l", [P, 3 * E], F32R)
        wo_full = sb("wo_full", [P, E])
        wqh, wql = sb("wqh", [P, DEPTH, 3 * INNER], F32R), sb("wql", [P, DEPTH, 3 * INNER], F32R)
        wuh, wul = sb("wuh", [P, DEPTH, 2, HT * P], F32R), sb("wul", [P, DEPTH, 2, HT * P], F32R)
        wo_local = sb("wo_local", [P, DEPTH, NPAIR, E])
        wd = sb("wd", [P, DEPTH, HT, E])
        bias3 = sb("bias3", [P, 3 * E])
        bo = sb("bo", [P, 1])
        lng, lnb, b2 = sb("lng", [P, DEPTH]), sb("lnb", [P, DEPTH]), sb("b2", [P, DEPTH])
        b1 = sb("b1", [P, DEPTH, 2, HT])
        ident, centre = sb("ident", [P, P]), sb("centre", [P, P])
        ones, mean_of = sb("ones", [P, P]), sb("mean_of", [P, 1])
        identb, mask = sb("identb", [P, P], BF16), sb("mask", [P, 2, P], BF16)
        half = sb("half", [P, NB])
        tab = sb("tab", [P, DEPTH, 2, 2, NB, LD])

        xt = sb("xt", [P, 2, NB, E])
        st, mv, mean = sb("st", [P, NB, 6]), sb("mv", [P, 3, NB]), sb("mean", [P, NB])
        ve4, rs4 = sb("ve4", [P, NB]), sb("rs4", [P, NB])
        xT = [sb(f"xT{c}", [P, S]) for c in range(2)]
        xh, xl = sb("xh", [P, S], F32R), sb("xl", [P, S], F32R)
        qkvf = sb("qkvf", [P, 2, NB, 3, H, D])
        pr = sb("pr", [P, H * H * D])
        sf, ef = sb("sf", [P, H, H]), sb("ef", [P, H, H])
        nmf, sumf, rf = sb("nmf", [P, H]), sb("sumf", [P, H]), sb("rf", [P, H])
        of, ofs = sb("of", [P, H, D]), sb("ofs", [P, 2, H, D])
        orow, oT = sb("orow", [P, NB, E]), sb("oT", [P, S])
        hh, hl = sb("hh", [P, S], F32R), sb("hl", [P, S], F32R)
        qk, sq = sb("qk", [P, 2, 1024]), sb("sq", [P, 2, 1024])
        ssq, rn = sb("ssq", [P, 2, 2, 16]), sb("rn", [P, 2, 16])
        t2 = sb("t2", [P, 2, 1024])
        qbd = sb("qbd", [P, 2, NPAIR, 2, 2, WIN])
        kT = sb("kT", [P, NPAIR, WIN + S])
        v, vs = sb("v", [P, NB, INNER]), sb("vs", [P, NB, INNER])
        nml, suml, rl = sb("nml", [P, 4, HW]), sb("suml", [P, 4, HW]), sb("rl", [P, 4, HW])
        pl = sb("pl", [P, 4, HW, P])
        pT = sb("pT", [P, 2, HW, P])
        oTl = sb("oTl", [P, NPAIR, S])
        x2, hs, hc, rs, sq2 = [sb(name, [P, S]) for name in ("x2", "hs", "hc", "rs", "sq2")]
        veps, rsq = sb("veps", [P, NB]), sb("rsq", [P, NB])
        mh, ml = sb("mh", [P, S], F32R), sb("ml", [P, S], F32R)
        gate, hid = sb("gate", [P, 2, S]), sb("hid", [P, HT, S])
        yT, rT, ob = sq2, hs, sb("ob", [P, NB, E])
        stage = pr[:]
        stage2 = [qk[:, :, :].rearrange("p a b -> p (a b)"), oTl[:, :, :].rearrange("p a b -> p (a b)")]
        stage3 = v[:, :, :].rearrange("p a b -> p (a b)")
        scale_rows = stage[:, 384:896].rearrange("p (l a k d) -> p l a k d", l=DEPTH, a=2, k=2)

        ring = [ctx.enter_context(nc.psum_tensor(f"ring{k}", [P, S], F32)) for k in range(RING)]
        scratch = nc.dram_tensor("heads_scratch", (H, S, D), F32, kind="Internal").ap()

        s_w = ctx.enter_context(nc.semaphore("weights_loaded"))
        s_set = ctx.enter_context(nc.semaphore("memory_set"))
        s_prep = ctx.enter_context(nc.semaphore("weights_split"))
        s_va = ctx.enter_context(nc.semaphore("constants_set"))
        s_x = [signal(f"x_loaded_{c}", ("load",), lambda step, c=c: step[1] == c, unit=16) for c in range(2)]
        s_xr = signal("x_again_loaded", ("load_again",), unit=16)
        s_store = signal("output_stored", ("final",), unit=16, ahead=16)
        s_stats = signal("stats_done", ("norm_x",), 4)
        s_rstd = signal("rstd_done", ("norm_x",))
        s_xn = signal("xn_done", ("norm_x",))
        s_xh = signal("x_high_done", ("norm_t",))
        s_xl = signal("x_low_done", ("norm_t",))
        s_fp = signal("full_products", ("product_full",))
        s_fs = signal("full_scores_steps", ("scores_full",), 3)
        s_exp = signal("full_exponentials", ("exp_full",), ahead=16)
        s_fv = signal("full_values_steps", ("values_full",), 5, ahead=1)
        s_heads = [signal(f"heads_stored_{k}", ("values_full",), lambda step, k=k: step[2] % 2 == k, unit=16, ahead=16) for k in range(2)]
        s_orow = signal("heads_loaded", ("attn_load",), unit=16, ahead=32)
        s_hh = signal("h_high_done", ("shift",))
        s_hl = signal("h_low_done", ("shift",))
        s_sq = signal("squares_done", ("project",))
        s_sin = signal("sine_products", ("rope",))
        s_rot = signal("rotary_products", ("rope",))
        s_ssq = signal("square_sums", ("rope",), 2, ahead=1)
        s_rope = signal("rope_steps", ("rope",), 3, ahead=1)
        s_vs = [signal(f"shifted_v_loaded_{b}", ("project",), lambda step, b=b: int(step[2] in (b - 1, b)), unit=16)
                for b in range(NB)]
        s_nml = signal("local_max_done", ("scores",))
        s_rl = signal("local_reciprocals", ("scale",))
        s_pl = signal("local_probs_scaled", ("scale",), ahead=1)
        s_hs = signal("h_shifted", ("out_local",))
        s_sq2 = signal("centred_squares", ("center",))
        s_rs = signal("mlp_rstd", ("variance",))
        s_diag = signal("rstd_diagonals", ("diagonal",))
        s_tn = signal("mlp_norm_steps", ("spread",), 2)
        s_mh = signal("mlp_high", ("spread",))
        filled = signal("ring_filled", BANKS, lambda step: BANKS[step[0]])
        taken_by = {who: signal(f"{who}_took_bank", BANKS, lambda step, who=who: sum(taker(step, k) == who for k in range(BANKS[step[0]])))
                    for who in ("act", "dve")}
        for s in (filled, *taken_by.values()):
            s.ahead = s.per
            s.first += s.per

        def bank(count, step, k=0):
            return ring[count.segment.number[step, k] % RING]

        def took(step, k=0):
            return taken_by[taker(step, k)].sem

        def taken(count, step, k=0):
            who = taker(step, k)
            return count(taken_by[who], step, sum(taker(step, q) == who for q in range(k + 1)))

        def user_before(count, step, k=0):
            return count.segment.fills[(count.segment.number[step, k] - RING) % len(count.segment.fills)]

        def took_before(count, step, k=0):
            return took(*user_before(count, step, k))

        def free(count, step, k=0):
            return taken(count, *user_before(count, step, k))

        x_pairs = t["x"].rearrange("(j c) (n p) e -> j c p n e", c=2, p=P)
        out_pairs = out.rearrange("(j c) (n p) e -> j c p n e", c=2, p=P)

        loads = [
            (ident[:], t["c_ident"]), (centre[:], t["c_centre"]),
            (identb[:], t["c_identb"]), (mask[:, :, :], t["c_mask"].rearrange("a p c -> p a c")),
            (stage[:, 0:128], t["WqT"]), (stage[:, 128:256], t["WkT"]), (stage[:, 256:384], t["WvT"]),
            (wo_full[:], t["WoT"]),
            (lng[:], t["ln_g"].rearrange("l p -> p l")), (lnb[:], t["ln_b"].rearrange("l p -> p l")),
            (b2[:], t["b2"].rearrange("l p -> p l")),
            (tab[:, 0, :, :, :, :].rearrange("p a b n d -> p (a b) n d"), t["c_rope"].rearrange("a (n p) d -> p a n d", p=P)),
            (tab[:, 1, :, :, :, :].rearrange("p a b n d -> p (a b) n d"), t["c_rope"].rearrange("a (n p) d -> p a n d", p=P)),
        ]
        for k, name in enumerate(("bq", "bk", "bv")):
            loads.append((bias3[:, k * E:(k + 1) * E], t[name].rearrange("(n e) -> n e", n=1).to_broadcast([P, E])))
        loads.append((bo[:], t["bo"].rearrange("(p n) -> p n", n=1)))
        for l in range(DEPTH):
            loads += [(stage2[l][:, 0:3 * INNER], t["wqkv"][l]),
                      (wo_local[:, l, :, :], t["wo"][l].rearrange("(n p) f -> p n f", p=P)),
                      (wd[:, l, 0:2, :], t["w2"][l, 0:256].rearrange("(n p) f -> p n f", p=P)),
                      (wd[0:HID - 256, l, 2, :], t["w2"][l, 256:HID])]
            for a in range(2):
                loads.append((stage3[:, (2 * l + a) * 384:(2 * l + a) * 384 + HID], t["w1"][l, :, a * HID:(a + 1) * HID]))
                loads.append((b1[:, l, a, 0:2], t["b1"][l, a * HID:a * HID + 256].rearrange("(n p) -> p n", p=P)))
                loads.append((b1[0:HID - 256, l, a, 2:3], t["b1"][l, a * HID + 256:(a + 1) * HID].rearrange("(p n) -> p n", n=1)))
            for k, name in enumerate(("q_scale", "k_scale")):
                row = t[name][l:l + 1, :]
                loads.append((scale_rows[:, l, 0, k, :], row.to_broadcast([P, LD])))
                loads.append((scale_rows[:, l, 1, k, 0:32], row[:, 32:64].to_broadcast([P, 32])))
                loads.append((scale_rows[:, l, 1, k, 32:64], row[:, 0:32].to_broadcast([P, 32])))
        LOADS = len(loads)

        def all_done(eng):
            for s in signals:
                if s.first > s.ahead:
                    eng.wait_ge(s.sem, s.first)

        block = ctx.enter_context(nc.Block())

        @block.sync
        def _(sp):
            sp.wait_ge(s_set, 3)
            for dst, src in loads:
                sp.dma_start(dst, src, allow_slow_non_contiguous=True).then_inc(s_w, 16)

            def run(count, this, following):
                for step in count.segment.steps:
                    kind, count.step = step[0], step
                    if kind == "load":
                        c = step[1]
                        sp.wait_ge(filled.sem, count(filled, ("norm_t", c)))
                        sp.dma_start(xt[:, c, :, :], x_pairs[following, c:c + 1].rearrange("j c p n e -> p (j c n) e")).then_inc(s_x[c].sem, 16)
                    if kind == "load_again":
                        c = step[1]
                        sp.wait_ge(s_store.sem, count(s_store, ("final", 1 - c)))
                        sp.dma_start(ob[:, :, :], x_pairs[this, c:c + 1].rearrange("j c p n e -> p (j c n) e")).then_inc(s_xr.sem, 16)
                    if kind == "values_full":
                        _, c, b = step
                        sp.wait_ge(s_fv.sem, count(s_fv, step, 5))
                        sp.dma_start(scratch.rearrange("h t d -> t h d")[b * P:(b + 1) * P], ofs[:, b % 2, :, :]).then_inc(s_heads[b % 2].sem, 16)
                    if kind == "project":
                        _, u, b = step
                        sp.wait_ge(took(step, 2), taken(count, step, 2))
                        sp.dma_start(vs[64:128, b, :], v[0:64, b, :]).then_inc(s_vs[b].sem, 16)
                        if b + 1 < NB:
                            sp.wait_ge(filled.sem, count(filled, ("values", (u - 1) % NU, 2 * b + 3)))
                            sp.dma_start(vs[0:64, b + 1, :], v[64:128, b, :]).then_inc(s_vs[b + 1].sem, 16)
                    if kind == "final":
                        c = step[1]
                        sp.wait_ge(took(step), taken(count, step))
                        sp.dma_start(out_pairs[this, c:c + 1].rearrange("j c p n e -> p (j c n) e"), ob[:, :, :]).then_inc(s_store.sem, 16)

            sp.wait_ge(s_prep, PREPS + 1)
            run(Count(BEFORE), None, slice(0, 1))
            all_done(sp)
            with sp.Fori(0, B // 2) as i:
                wrapped = sp.alloc_register("following_pair")
                sp.reg_alu(wrapped, i, 1, ALU.add)
                sp.reg_alu(wrapped, wrapped, B // 2 - 1, ALU.bitwise_and)
                run(Count(PASS, sp, i, signals), bass.ds(i, 1), bass.ds(sp.snap(wrapped), 1))
            sp.wait_ge(s_store.sem, s_store.ahead + B // 2 * s_store.per)
            for s in s_heads:
                sp.wait_ge(s.sem, s.first + B // 2 * s.per)
            for s in s_vs:
                sp.wait_ge(s.sem, s.first + B // 2 * s.per)

        @block.gpsimd
        def _(pool):
            nc.gpsimd.memset(half[:], -0.5).then_inc(s_va, 1)
            nc.gpsimd.memset(ones[:], 1.0).then_inc(s_va, 1)
            nc.gpsimd.memset(mean_of[:], 1.0 / E).then_inc(s_va, 1)
            nc.gpsimd.memset(vs[:, 0, :], 0.0).then_inc(s_va, 1)
            nc.gpsimd.memset(kT[:, :, 0:WIN], 0.0).then_inc(s_va, 1)

            def run(count):
                for step in count.segment.steps:
                    kind, count.step = step[0], step
                    if kind == "norm_x":
                        pool.wait_ge(s_stats.sem, count(s_stats, step, 4))
                        nc.gpsimd.tensor_tensor(rs4[:], ve4[:], half[:], ALU.pow).then_inc(s_rstd.sem, 1)
                    if kind == "rope":
                        _, u, b = step
                        q = qk[:, b % 2, :]
                        qh3 = q.rearrange("p (h d) -> p h d", d=LD)
                        pool.wait_ge(s_rot.sem, count(s_rot, step))
                        nc.gpsimd.tensor_tensor(q, q, t2[:, b % 2, :], ALU.add).then_inc(s_rope.sem, 1)
                        pool.wait_ge(s_ssq.sem, count(s_ssq, step, 2))
                        nc.gpsimd.tensor_tensor(rn[:, b % 2, :], ssq[:, b % 2, 1, :], half[:, 0:1].to_broadcast([P, 16]), ALU.pow).then_inc(s_rope.sem, 1)
                        pool.wait_ge(s_rope.sem, count(s_rope, step, 2))
                        nc.gpsimd.tensor_tensor(qh3, qh3, rn[:, b % 2, :, None].to_broadcast([P, 16, LD]), ALU.mult).then_inc(s_rope.sem, 1)
                    if kind == "product_full":
                        _, c, b = step
                        q, k = (qkvf[:, c, b, n, :, :] for n in range(2))
                        pool.wait_ge(took(("qkv_full", c, b)), taken(count, ("qkv_full", c, b)))
                        pool.wait_ge(s_fv.sem, count(s_fv, full_before(step, 1), 5))
                        nc.gpsimd.tensor_tensor(pr[:].rearrange("p (q k d) -> p q k d", q=H, k=H), q[:, :, None, :].to_broadcast([P, H, H, D]),
                                                k[:, None, :, :].to_broadcast([P, H, H, D]), ALU.mult).then_inc(s_fp.sem, 1)
                    if kind == "scale":
                        d = step[2]
                        pool.wait_ge(s_rl.sem, count(s_rl, step))
                        pb = pl[:, d % 4, :, :]
                        nc.gpsimd.tensor_tensor(pb, pb, rl[:, d % 4, :, None].to_broadcast([P, HW, P]), ALU.mult).then_inc(s_pl.sem, 1)
                    if kind == "variance":
                        pool.wait_ge(took(step), taken(count, step))
                        nc.gpsimd.tensor_tensor(rsq[:], veps[:], half[:], ALU.pow).then_inc(s_rs.sem, 1)

            pool.wait_ge(s_va, 5)
            run(Count(BEFORE))
            all_done(pool)
            with pool.Fori(0, B // 2) as i:
                run(Count(PASS, pool, i, signals))

        @block.scalar
        def _(act):
            def copy(dst, src):
                return nc.scalar.activation(dst, src, ACT.Copy)

            def run(count):
                for step in count.segment.steps:
                    kind, count.step = step[0], step
                    if kind == "norm_t":
                        c = step[1]
                        act.wait_ge(filled.sem, count(filled, step))
                        copy(xT[c][:], bank(count, step)[:]).then_inc(took(step), 1)
                        act.wait_ge(took(step), taken(count, step))
                        act.wait_ge(filled.sem, count(filled, ("qkv_full", 1 - c, NB - 1)))
                        copy(xh[:], xT[c][:]).then_inc(s_xh.sem, 1)
                    if kind == "shift":
                        u = step[1]
                        src = xT[u % 2]
                        if u < 2:
                            act.wait_ge(took(("norm_t", u)), taken(count, ("norm_t", u)))
                        else:
                            act.wait_ge(took(("down", u - 2)), taken(count, ("down", u - 2)))
                        act.wait_ge(filled.sem, count(filled, ("project", (u - 1) % NU, NB - 1), 3))
                        copy(hh[0:64, :], src[0:64, :])
                        copy(hh[64:128, 1:S], src[64:128, 0:S - 1]).then_inc(s_hh.sem, 1)
                    if kind == "project":
                        _, u, b = step
                        for k in range(2):
                            act.wait_ge(filled.sem, count(filled, step, k + 1))
                            if k == 0:
                                act.wait_ge(filled.sem, count(filled, ("qk_t",) + back(step, 2, NB)[1:], 2))
                            copy(qk[:, b % 2, k * 512:(k + 1) * 512], bank(count, step, k)[:]).then_inc(took(step, k), 1)
                        act.wait_ge(took(step, 1), taken(count, step, 1))
                        act.wait_ge(s_ssq.sem, count(s_ssq, ("rope",) + back(step, 2, NB)[1:], 1))
                        nc.scalar.activation(sq[:, b % 2, :], qk[:, b % 2, :], ACT.Square).then_inc(s_sq.sem, 1)
                        act.wait_ge(filled.sem, count(filled, step, 3))
                        act.wait_ge(filled.sem, count(filled, ("values", (u - 1) % NU, min(2 * b + 3, 7))))
                        copy(v[:, b, :], bank(count, step, 2)[:]).then_inc(took(step, 2), 1)
                    if kind == "qk_t":
                        _, u, b = step
                        act.wait_ge(filled.sem, count(filled, step, 1))
                        ps = bank(count, step, 0)[:, :].rearrange("p (a w i) -> p a w i", a=NPAIR, w=2)
                        before = back(step, 2, NB)
                        act.wait_ge(filled.sem, count(filled, ("scores", before[1], 2 * before[2] + 1)))
                        copy(qbd[0:64, b % 2, :, :, 0, :], ps[0:64])
                        copy(qbd[64:128, b % 2, :, :, 1, :], ps[64:128]).then_inc(took(step, 0), 1)
                    if kind == "scores":
                        d = step[2]
                        act.wait_ge(s_nml.sem, count(s_nml, step))
                        act.wait_ge(filled.sem, count(filled, ("probs_t",) + back(step, 4, 8)[1:]))
                        for k in range(HW):
                            last = nc.scalar.activation(pl[:, d % 4, k, :], bank(count, step)[:, k * P:(k + 1) * P], ACT.Exp,
                                                        bias=nml[:, d % 4, k:k + 1], accum_out=suml[:, d % 4, k:k + 1])
                        last.then_inc(took(step), 1)
                    if kind == "probs_t":
                        act.wait_ge(filled.sem, count(filled, step))
                        act.wait_ge(filled.sem, count(filled, ("values",) + back(step, 2, 8)[1:]))
                        copy(pT[:, step[2] % 2, :, :], bank(count, step)[:, :].rearrange("p (a b) -> p a b", a=HW)).then_inc(took(step), 1)
                    if kind == "values":
                        act.wait_ge(filled.sem, count(filled, step))
                        _, u, d = step
                        b, pair = d // 2, 2 * (d % 2)
                        ps = bank(count, step)[:, :].rearrange("p (a w h i) -> p a w h i", a=2, w=2, h=2)
                        dst = oTl[:, pair:pair + 2, b * P:(b + 1) * P].rearrange("p a (w i) -> p a w i", w=2)
                        copy(dst[0:64], ps[0:64, :, :, 0, :])
                        copy(dst[64:128], ps[64:128, :, :, 1, :]).then_inc(took(step), 1)
                    if kind == "out_local":
                        act.wait_ge(took(step), taken(count, step))
                        copy(hs[0:64, :], x2[0:64, :])
                        copy(hs[64:128, 1:S], x2[64:128, 0:S - 1]).then_inc(s_hs.sem, 1)
                    if kind == "center":
                        act.wait_ge(filled.sem, count(filled, step))
                        copy(hc[:], bank(count, step)[:]).then_inc(took(step), 1)
                        act.wait_ge(took(step), taken(count, step))
                        nc.scalar.activation(sq2[:], hc[:], ACT.Square).then_inc(s_sq2.sem, 1)
                    if kind == "spread":
                        act.wait_ge(s_tn.sem, count(s_tn, step, 1))
                        copy(mh[:], hc[:]).then_inc(s_mh.sem, 1)
                    if kind == "up":
                        _, u, c = step
                        act.wait_ge(filled.sem, count(filled, step, 1))
                        if c >= 2:
                            act.wait_ge(took(("up", u, c - 2), 1), taken(count, ("up", u, c - 2), 1))
                        nc.scalar.activation(gate[:, c % 2, :], bank(count, step, 0)[:], ACT.Gelu, bias=b1[:, u // 2, 1, c:c + 1]).then_inc(took(step, 0), 1)
                    if kind == "exp_full":
                        act.wait_ge(s_fs.sem, count(s_fs, ("scores_full",) + step[1:], 3))
                        nc.scalar.activation(ef[:, :, :], sf[:, :, :], ACT.Exp, scale=SCALE).then_inc(s_exp.sem, 1)
                    if kind == "attn_load":
                        c = step[1]
                        for k in range(2):
                            act.wait_ge(s_heads[k].sem, count(s_heads[k], ("values_full", c, NB - 2 + k)))
                        act.wait_ge(filled.sem, count(filled, ("attn_t", 1 - c)))
                        act.dma_start(orow[:, :, :], scratch.rearrange("h (a t) d -> (h a) (t d)", t=E // D)
                                     .rearrange("(n p) e -> p n e", p=P)).then_inc(s_orow.sem, 16)
                    if kind == "attn_t":
                        act.wait_ge(filled.sem, count(filled, step))
                        copy(oT[:], bank(count, step)[:]).then_inc(took(step), 1)

            act.wait_ge(s_w, 16 * LOADS)
            act.wait_ge(s_prep, PREPS + 1)
            run(Count(BEFORE))
            all_done(act)
            with act.Fori(0, B // 2) as i:
                run(Count(PASS, act, i, signals))

        @block.vector
        def _(dve):
            nc.vector.memset(wd[:, :, :, :], 0.0).then_inc(s_set, 1)
            nc.vector.memset(b1[:, :, :, :], 0.0).then_inc(s_set, 1)
            nc.vector.memset(stage3, 0.0).then_inc(s_set, 1)
            dve.wait_ge(s_w, 16 * LOADS)
            n = 0
            for dsth, dstl, src in ((w3h[:], w3l[:], stage[:, 0:384]),
                                    (wqh[:, 0, :], wql[:, 0, :], stage2[0][:, 0:3 * INNER]),
                                    (wqh[:, 1, :], wql[:, 1, :], stage2[1][:, 0:3 * INNER]),
                                    (wuh[:, :, :, :], wul[:, :, :, :], stage3[:, 0:1536].rearrange("p (a b c) -> p a b c", a=2, b=2))):
                nc.vector.tensor_copy(dsth, src).then_inc(s_prep, 1)
                n += 1
                dve.wait_ge(s_prep, n)
                nc.vector.tensor_tensor(dstl, src, dsth.bitcast(F32), ALU.subtract).then_inc(s_prep, 1)
                n += 1
            for l in range(DEPTH):
                for a in range(2):
                    for k in range(2):
                        nc.vector.tensor_tensor(tab[:, l, a, k, :, :], tab[:, l, a, k, :, :],
                                                scale_rows[:, l, a, k, None, :].to_broadcast([P, NB, LD]),
                                                ALU.mult).then_inc(s_prep, 1)
                        n += 1
            dve.wait_ge(s_prep, n)
            assert n == PREPS
            for part in (hh, hl):
                nc.vector.memset(part[64:128, 0:1].bitcast(F32), 0.0)
            for s in signals:
                if s.ahead:
                    nc.vector.memset(of[:, :, :], 0.0).then_inc(s.sem, s.ahead)
                    dve.wait_ge(s.sem, s.ahead)
            nc.vector.memset(qbd[:, :, :, :, :, :], 0.0).then_inc(s_prep, 1)
            dve.wait_ge(s_prep, n + 1)

            def copy(dst, src):
                return nc.vector.tensor_copy(dst, src)

            def run(count):
                for step in count.segment.steps:
                    kind, count.step = step[0], step
                    if kind == "norm_x":
                        c = step[1]
                        x = xt[:, c, :, :]
                        dve.wait_ge(s_x[c].sem, count(s_x[c], ("load", c)))
                        for b in range(NB):
                            last = nc.vector.bn_stats(st[:, b, :], x[:, b, :])
                        last.then_inc(s_stats.sem, 1)
                        me, se, mo, so = (st[:, :, k] for k in (1, 2, 4, 5))
                        dve.wait_ge(s_stats.sem, count(s_stats, step, 1))
                        nc.vector.tensor_tensor(mv[:, 0, :], me, mo, ALU.add)
                        nc.vector.tensor_tensor(mv[:, 1, :], me, mo, ALU.subtract)
                        nc.vector.tensor_tensor(mv[:, 2, :], se, so, ALU.add).then_inc(s_stats.sem, 1)
                        dve.wait_ge(s_stats.sem, count(s_stats, step, 2))
                        nc.vector.tensor_scalar(mean[:], mv[:, 0, :], 0.5, None, ALU.mult)
                        nc.vector.tensor_tensor(mv[:, 1, :], mv[:, 1, :], mv[:, 1, :], ALU.mult)
                        nc.vector.tensor_scalar(mv[:, 2, :], mv[:, 2, :], 1.0 / E, EPS, ALU.mult, ALU.add).then_inc(s_stats.sem, 1)
                        dve.wait_ge(s_stats.sem, count(s_stats, step, 3))
                        nc.vector.scalar_tensor_tensor(ve4[:], mv[:, 1, :], 0.25, mv[:, 2, :], ALU.mult, ALU.add).then_inc(s_stats.sem, 1)
                        dve.wait_ge(s_rstd.sem, count(s_rstd, step))
                        for b in range(NB):
                            last = nc.vector.tensor_scalar(x[:, b, :], x[:, b, :], mean[:, b:b + 1], rs4[:, b:b + 1],
                                                           ALU.subtract, ALU.mult)
                        last.then_inc(s_xn.sem, 1)
                    if kind == "norm_t":
                        c = step[1]
                        dve.wait_ge(s_xh.sem, count(s_xh, step))
                        nc.vector.tensor_tensor(xl[:], xT[c][:], xh[:].bitcast(F32), ALU.subtract).then_inc(s_xl.sem, 1)
                    if kind == "shift":
                        src = xT[step[1] % 2]
                        dve.wait_ge(s_hh.sem, count(s_hh, step))
                        nc.vector.tensor_tensor(hl[0:64, :], src[0:64, :], hh[0:64, :].bitcast(F32), ALU.subtract)
                        nc.vector.tensor_tensor(hl[64:128, 1:S], src[64:128, 0:S - 1], hh[64:128, 1:S].bitcast(F32),
                                                ALU.subtract).then_inc(s_hl.sem, 1)
                    if kind == "qkv_full":
                        _, c, b = step
                        dve.wait_ge(filled.sem, count(filled, step))
                        dve.wait_ge(s_fv.sem, count(s_fv, ("values_full", c, b), 5))
                        nc.vector.tensor_tensor(qkvf[:, c, b, :, :, :].rearrange("p k h d -> p (k h d)"), bank(count, step)[:, 0:3 * E],
                                                bias3[:], ALU.add).then_inc(took(step), 1)
                    if kind == "scores_full":
                        _, c, b = step
                        dve.wait_ge(s_fp.sem, count(s_fp, ("product_full", c, b)))
                        nc.vector.reduce_sum(sf[:, :, :], pr[:].rearrange("p (q k d) -> p q k d", q=H, k=H), AX_X).then_inc(s_fs.sem, 1)
                        dve.wait_ge(s_fs.sem, count(s_fs, step, 1))
                        nc.vector.tensor_reduce(nmf[:], sf[:, :, :], AX_X, ALU.max, negate=True).then_inc(s_fs.sem, 1)
                        dve.wait_ge(s_fs.sem, count(s_fs, step, 2))
                        nc.vector.tensor_tensor(sf[:, :, :], sf[:, :, :], nmf[:, :, None].to_broadcast([P, H, H]), ALU.add).then_inc(s_fs.sem, 1)
                    if kind == "values_full":
                        _, c, b = step
                        pr4 = pr[:].rearrange("p (q d k) -> p q d k", q=H, d=D)
                        vt = qkvf[:, c, b, 2, :, :].rearrange("p k d -> p d k")
                        dve.wait_ge(s_exp.sem, count(s_exp, ("exp_full", c, b)))
                        nc.vector.tensor_tensor(pr4, ef[:, :, None, :].to_broadcast([P, H, D, H]), vt[:, None, :, :].to_broadcast([P, H, D, H]),
                                                ALU.mult).then_inc(s_fv.sem, 1)
                        nc.vector.reduce_sum(sumf[:], ef[:, :, :], AX_X).then_inc(s_fv.sem, 1)
                        dve.wait_ge(s_fv.sem, count(s_fv, step, 2))
                        nc.vector.reduce_sum(of[:, :, :], pr4, AX_X).then_inc(s_fv.sem, 1)
                        nc.vector.reciprocal(rf[:], sumf[:]).then_inc(s_fv.sem, 1)
                        dve.wait_ge(s_fv.sem, count(s_fv, step, 4))
                        if b == 0:
                            dve.wait_ge(s_orow.sem, count(s_orow, ("attn_load", 1 - c)))
                        dve.wait_ge(s_heads[b % 2].sem, count(s_heads[b % 2], full_before(step, 2)))
                        nc.vector.tensor_tensor(ofs[:, b % 2, :, :], of[:, :, :], rf[:, :, None].to_broadcast([P, H, D]), ALU.mult).then_inc(s_fv.sem, 1)
                    if kind == "rope":
                        _, u, b = step
                        q4 = qk[:, b % 2, :].rearrange("p (a h d) -> p a h d", a=2, h=LH)
                        cos = tab[:, u // 2, 0, :, b, None, :].to_broadcast([P, 2, LH, LD])
                        sin = tab[:, u // 2, 1, :, b, None, :]
                        dve.wait_ge(took(("project", u, b), 1), taken(count, ("project", u, b), 1))
                        dve.wait_ge(s_rope.sem, count(s_rope, back(step, 2, NB), 3))
                        t24 = t2[:, b % 2, :].rearrange("p (a h d) -> p a h d", a=2, h=LH)
                        for k in range(2):
                            o, s_ = 32 * k, 32 - 32 * k
                            last = nc.vector.tensor_tensor(t24[:, :, :, o:o + 32], q4[:, :, :, s_:s_ + 32],
                                                           sin[:, :, :, o:o + 32].to_broadcast([P, 2, LH, 32]), ALU.mult)
                        last.then_inc(s_sin.sem, 1)
                        dve.wait_ge(s_sin.sem, count(s_sin, step))
                        dve.wait_ge(s_sq.sem, count(s_sq, ("project", u, b)))
                        nc.vector.tensor_tensor(q4, q4, cos, ALU.mult).then_inc(s_rot.sem, 1)
                        nc.vector.reduce_sum(ssq[:, b % 2, 0, :], sq[:, b % 2, :].rearrange("p (h d) -> p h d", d=LD), AX_X).then_inc(s_ssq.sem, 1)
                        dve.wait_ge(s_ssq.sem, count(s_ssq, step, 1))
                        nc.vector.tensor_scalar(ssq[:, b % 2, 1, :], ssq[:, b % 2, 0, :], TINY, None, ALU.max).then_inc(s_ssq.sem, 1)
                    if kind == "qk_t":
                        b = step[2]
                        dve.wait_ge(filled.sem, count(filled, step, 2))
                        copy(kT[:, :, WIN + P * b:WIN + P * b + P],
                             bank(count, step, 1)[:, :].rearrange("p (a c) -> p a c", a=NPAIR)).then_inc(took(step, 1), 1)
                    if kind == "scores":
                        d = step[2]
                        dve.wait_ge(filled.sem, count(filled, step))
                        nc.vector.tensor_reduce(nml[:, d % 4, :], bank(count, step)[:, :].rearrange("p (a b) -> p a b", a=HW), AX_X,
                                                ALU.max, negate=True).then_inc(s_nml.sem, 1)
                    if kind == "scale":
                        _, u, d = step
                        dve.wait_ge(s_pl.sem, count(s_pl, back(step, 4, 8)))
                        dve.wait_ge(took(("scores", u, d)), taken(count, ("scores", u, d)))
                        nc.vector.reciprocal(rl[:, d % 4, :], suml[:, d % 4, :]).then_inc(s_rl.sem, 1)
                    if kind == "out_local":
                        u = step[1]
                        dve.wait_ge(filled.sem, count(filled, step))
                        nc.vector.memset(hs[64:128, 0:1], 0.0)
                        nc.vector.tensor_tensor(x2[:], bank(count, step)[:], xT[u % 2][:], ALU.add).then_inc(took(step), 1)
                    if kind == "variance":
                        dve.wait_ge(filled.sem, count(filled, step))
                        nc.vector.tensor_scalar(veps[:], bank(count, step)[:, 0:NB], EPS, None, ALU.add).then_inc(took(step), 1)
                    if kind == "diagonal":
                        dve.wait_ge(s_rs.sem, count(s_rs, ("variance", step[1])))
                        for b in range(NB):
                            last = nc.vector.tensor_scalar(rs[:, b * P:(b + 1) * P], ident[:], rsq[:, b:b + 1], None, ALU.mult)
                        last.then_inc(s_diag.sem, 1)
                    if kind == "spread":
                        l = step[1] // 2
                        dve.wait_ge(filled.sem, count(filled, step))
                        nc.vector.tensor_tensor(hc[:], hc[:], bank(count, step)[:], ALU.mult).then_inc(took(step), 1)
                        dve.wait_ge(took(step), taken(count, step))
                        nc.vector.tensor_scalar(hc[:], hc[:], lng[:, l:l + 1], lnb[:, l:l + 1], ALU.mult, ALU.add).then_inc(s_tn.sem, 1)
                        dve.wait_ge(s_mh.sem, count(s_mh, step))
                        nc.vector.tensor_tensor(ml[:], hc[:], mh[:].bitcast(F32), ALU.subtract).then_inc(s_tn.sem, 1)
                    if kind == "up":
                        _, u, c = step
                        dve.wait_ge(filled.sem, count(filled, step, 2))
                        dve.wait_ge(took(step, 0), taken(count, step, 0))
                        nc.vector.scalar_tensor_tensor(hid[:, c, :], bank(count, step, 1)[:], b1[:, u // 2, 0, c:c + 1], gate[:, c % 2, :],
                                                       ALU.add, ALU.mult).then_inc(took(step, 1), 1)
                    if kind == "down":
                        u = step[1]
                        to = yT if u >= NU - 2 else xT[u % 2]
                        dve.wait_ge(filled.sem, count(filled, step))
                        nc.vector.scalar_tensor_tensor(to[:], bank(count, step)[:], b2[:, u // 2:u // 2 + 1], x2[:],
                                                       ALU.add, ALU.add).then_inc(took(step), 1)
                    if kind == "attn_out":
                        down = ("down", NU - 2 + step[1])
                        dve.wait_ge(filled.sem, count(filled, step))
                        dve.wait_ge(took(down), taken(count, down))
                        nc.vector.scalar_tensor_tensor(rT[:], bank(count, step)[:], bo[:], yT[:], ALU.add, ALU.add).then_inc(took(step), 1)
                    if kind == "final":
                        dve.wait_ge(filled.sem, count(filled, step))
                        dve.wait_ge(s_xr.sem, count(s_xr, ("load_again", step[1])))
                        nc.vector.tensor_tensor(ob[:, :, :], bank(count, step)[:, :].rearrange("p (n e) -> p n e", n=NB), ob[:, :, :],
                                                ALU.add).then_inc(took(step), 1)

            run(Count(BEFORE))
            all_done(dve)
            with dve.Fori(0, B // 2) as i:
                run(Count(PASS, dve, i, signals))

        @block.tensor
        def _(pe):
            mm = nc.tensor.matmul

            def parts3(dst, ah, al, bh, bl):
                mm(dst, ah, bh, start=True, stop=False)
                mm(dst, ah, bl, start=False, stop=False)
                return mm(dst, al, bh, start=False, stop=True)

            def run(count):
                def claim(step, k=0):
                    return took_before(count, step, k), free(count, step, k)

                for step in count.segment.steps:
                    kind, count.step = step[0], step
                    ps = bank(count, step) if kind in BANKS else None
                    if kind == "norm_t":
                        c = step[1]
                        pe.wait_ge(*claim(step))
                        pe.wait_ge(s_xn.sem, count(s_xn, ("norm_x", c)))
                        for b in range(NB):
                            last = nc.tensor.transpose(ps[:, b * P:(b + 1) * P], xt[:, c, b, :], ident[:])
                        last.then_inc(filled.sem, 1)
                    if kind == "qkv_full":
                        _, c, b = step
                        pe.wait_ge(*claim(step))
                        pe.wait_ge(s_xl.sem, count(s_xl, ("norm_t", c)))
                        o = slice(b * P, (b + 1) * P)
                        parts3(ps[:, 0:3 * E], xh[:, o], xl[:, o], w3h[:], w3l[:]).then_inc(filled.sem, 1)
                    if kind == "project":
                        _, u, b = step
                        pe.wait_ge(s_hl.sem, count(s_hl, ("shift", u)))
                        c = slice(b * P, (b + 1) * P)
                        for k in range(3):
                            o = slice(k * INNER, (k + 1) * INNER)
                            pe.wait_ge(*claim(step, k))
                            parts3(bank(count, step, k)[:], hh[:, c], hl[:, c], wqh[:, u // 2, o], wql[:, u // 2, o]).then_inc(filled.sem, 1)
                    if kind == "qk_t":
                        _, u, b = step
                        pe.wait_ge(s_rope.sem, count(s_rope, ("rope", u, b), 3))
                        for k in range(2):
                            pe.wait_ge(*claim(step, k))
                            ps = bank(count, step, k)
                            for a in range(NPAIR):
                                last = nc.tensor.transpose(ps[:, a * P:(a + 1) * P], qk[:, b % 2, k * 512 + a * P:k * 512 + (a + 1) * P], ident[:])
                            last.then_inc(filled.sem, 1)
                    if kind == "scores":
                        _, u, d = step
                        b = d // 2
                        for k in range(2):
                            pe.wait_ge(took(("qk_t", u, b), k), taken(count, ("qk_t", u, b), k))
                        pe.wait_ge(*claim(step))
                        for k in range(4):
                            pair, wi = 2 * (d % 2) + k // 2, 2 * b + k % 2
                            o = ps[:, k * P:(k + 1) * P]
                            mm(o, qbd[:, b % 2, pair, k % 2, :, :].rearrange("p a b -> p (a b)"), kT[:, pair, WIN * wi:WIN * wi + P], start=True, stop=False)
                            last = mm(o, identb[:], mask[:, int(wi == 0), :], start=False, stop=True)
                        last.then_inc(filled.sem, 1)
                    if kind == "probs_t":
                        _, u, d = step
                        pe.wait_ge(s_pl.sem, count(s_pl, ("scale", u, d)))
                        pe.wait_ge(*claim(step))
                        for k in range(HW):
                            last = nc.tensor.transpose(ps[:, k * P:(k + 1) * P], pl[:, d % 4, k, :], ident[:])
                        last.then_inc(filled.sem, 1)
                    if kind == "values":
                        _, u, d = step
                        b = d // 2
                        pe.wait_ge(took(("probs_t", u, d)), taken(count, ("probs_t", u, d)))
                        if d % 2 == 0:
                            pe.wait_ge(s_vs[b].sem, count(s_vs[b], ("project", u, b)))
                        pe.wait_ge(*claim(step))
                        for k in range(4):
                            pair = 2 * (d % 2) + k // 2
                            vals = v[:, b, :] if k % 2 else vs[:, b, :]
                            last = mm(ps[:, k * P:(k + 1) * P], vals[:, pair * P:(pair + 1) * P], pT[:, d % 2, k, :], start=True, stop=True)
                        last.then_inc(filled.sem, 1)
                    if kind == "out_local":
                        u = step[1]
                        for d in (6, 7):
                            pe.wait_ge(took(("values", u, d)), taken(count, ("values", u, d)))
                        pe.wait_ge(*claim(step))
                        for a in range(NPAIR):
                            last = mm(ps[:], wo_local[:, u // 2, a, :], oTl[:, a, :], start=a == 0, stop=a == NPAIR - 1)
                        last.then_inc(filled.sem, 1)
                    if kind == "center":
                        pe.wait_ge(s_hs.sem, count(s_hs, ("out_local", step[1])))
                        pe.wait_ge(*claim(step))
                        mm(ps[:], centre[:], hs[:], start=True, stop=True).then_inc(filled.sem, 1)
                    if kind == "variance":
                        pe.wait_ge(s_sq2.sem, count(s_sq2, ("center", step[1])))
                        pe.wait_ge(*claim(step))
                        for b in range(NB):
                            last = mm(ps[:, b:b + 1], sq2[:, b * P:(b + 1) * P], mean_of[:], start=True, stop=True)
                        last.then_inc(filled.sem, 1)
                    if kind == "spread":
                        pe.wait_ge(s_diag.sem, count(s_diag, ("diagonal", step[1])))
                        pe.wait_ge(*claim(step))
                        mm(ps[:], ones[:], rs[:], start=True, stop=True).then_inc(filled.sem, 1)
                    if kind == "up":
                        _, u, c = step
                        if c == 0:
                            pe.wait_ge(s_tn.sem, count(s_tn, ("spread", u), 2))
                        for k in range(2):
                            o = slice(c * P, (c + 1) * P)
                            pe.wait_ge(*claim(step, k))
                            parts3(bank(count, step, k)[:], wuh[:, u // 2, 1 - k, o], wul[:, u // 2, 1 - k, o], mh[:], ml[:]).then_inc(filled.sem, 1)
                    if kind == "down":
                        u = step[1]
                        pe.wait_ge(took(("up", u, HT - 1), 1), taken(count, ("up", u, HT - 1), 1))
                        pe.wait_ge(*claim(step))
                        for c in range(HT):
                            last = mm(ps[:], wd[:, u // 2, c, :], hid[:, c, :], start=c == 0, stop=c == HT - 1)
                        last.then_inc(filled.sem, 1)
                    if kind == "attn_t":
                        pe.wait_ge(s_orow.sem, count(s_orow, ("attn_load", step[1])))
                        pe.wait_ge(*claim(step))
                        for b in range(NB):
                            last = nc.tensor.transpose(ps[:, b * P:(b + 1) * P], orow[:, b, :], ident[:])
                        last.then_inc(filled.sem, 1)
                    if kind == "attn_out":
                        pe.wait_ge(took(("attn_t", step[1])), taken(count, ("attn_t", step[1])))
                        pe.wait_ge(*claim(step))
                        mm(ps[:], wo_full[:], oT[:], start=True, stop=True).then_inc(filled.sem, 1)
                    if kind == "final":
                        pe.wait_ge(took(("attn_out", step[1])), taken(count, ("attn_out", step[1])))
                        pe.wait_ge(*claim(step))
                        for b in range(NB):
                            last = nc.tensor.transpose(ps[:, b * P:(b + 1) * P], rT[:, b * P:(b + 1) * P], ident[:])
                        last.then_inc(filled.sem, 1)

            pe.wait_ge(s_w, 16 * LOADS)
            pe.wait_ge(s_prep, PREPS + 1)
            pe.wait_ge(s_va, 5)
            run(Count(BEFORE))
            all_done(pe)
            with pe.Fori(0, B // 2) as i:
                run(Count(PASS, pe, i, signals))


def constants():
    import numpy as np

    f = np.float32
    i, c = np.arange(P)[:, None] % WIN, np.arange(P)[None, :]
    allowed = (i <= c) & (c <= i + WIN)
    masks = np.stack([np.where(allowed, 0.0, MASKED), np.where(allowed & (c >= WIN), 0.0, MASKED)])
    half_idx = np.arange(0, LD, 2, dtype=f)
    pos = np.arange(S, dtype=f)
    freqs = pos[:, None] * (f(1.0) / f(10000.0) ** (half_idx / f(LD)))[None, :]
    freqs = np.concatenate([freqs, freqs], axis=-1).astype(f)
    base = (half_idx + f(0.4 * LD)) / f(1.4 * LD)
    scale = base[None, :] ** ((pos - f(S // 2)) / f(WIN // 2))[:, None]
    scale = np.concatenate([scale, scale], axis=-1).astype(f)
    sign = np.where(np.arange(LD) < LD // 2, f(-1.0), f(1.0))
    cos, sin = np.cos(freqs), np.sin(freqs) * sign
    rope = np.stack([cos * scale * f(QK_SCALE), cos / scale, sin * scale * f(QK_SCALE), sin / scale])
    bf16 = mybir.dt.np(BF16)
    return {
        "c_ident": np.eye(P, dtype=f), "c_centre": (np.eye(P) - 1.0 / P).astype(f),
        "c_identb": np.eye(P).astype(bf16), "c_mask": masks.astype(bf16), "c_rope": rope.astype(f),
    }


def kernel(**inputs):
    import numpy as np
    from concourse import bacc
    from concourse.bass_utils import run_bass_kernel_spmd

    full, local = "L0_attn_", "L0_ffn_"
    arrays = {"x": inputs[full + "x"]}
    for name in ("Wq", "Wk", "Wv", "Wo"):
        arrays[name + "T"] = np.ascontiguousarray(np.asarray(inputs[full + name]).T)
    for name in ("bq", "bk", "bv", "bo"):
        arrays[name] = inputs[full + name]
    for name in ("wqkv", "q_scale", "k_scale", "wo", "ln_g", "ln_b", "w1", "b1", "w2", "b2"):
        arrays[name] = inputs[local + name]
    arrays = {k: np.ascontiguousarray(a) for k, a in arrays.items()} | constants()
    nc = bacc.Bacc("TRN2", target_bir_lowering=False, num_devices=1)
    t = {k: nc.dram_tensor(k, a.shape, mybir.dt.from_np(a.dtype), kind="ExternalInput").ap() for k, a in arrays.items()}
    out = nc.dram_tensor("out", (B, S, E), F32, kind="ExternalOutput").ap()
    build(nc, t, out)
    r = run_bass_kernel_spmd(nc, [arrays], core_ids=[0])
    return r.results[0]["out"]
```
